# Optimizing a Trainium2 kernel written in Bass

```python
import numpy as np
import jax
import jax.numpy as jnp

def _softmax(x, axis=-1):
    return jax.nn.softmax(x, axis=axis)
def _gelu(x):
    return jax.nn.gelu(x, approximate=True)
def _silu(x):
    return jax.nn.silu(x)
def _sigmoid(x):
    return jax.nn.sigmoid(x)
def _layernorm(x, axis=-1, eps=1e-5):
    m = jnp.mean(x, axis=axis, keepdims=True)
    v = jnp.var(x, axis=axis, keepdims=True)
    return (x - m) / jnp.sqrt(v + eps)
def _scatter_add(tgt, idx, src, axis=0):
    return tgt.at[idx].add(src)
def _segment_sum(src, seg, n):
    return jax.ops.segment_sum(src, seg, n)

kernel_name = 'mk_adj_preln_d1_adj_512_47839d'

def setup_inputs(seed: int = 0):
    np.random.seed(seed)
    _w = jnp.asarray
    def _rec_inputs():
        import jax
        import jax.numpy as jnp
        _gk = jax.random.key(seed)
        x = -0.0005963 + 1.001 * jax.random.normal(jax.random.fold_in(_gk, 1), (6144, 512), jnp.float32)
        _a = jax.random.bernoulli(jax.random.fold_in(_gk, 2), 0.000651042, (6144, 6144))
        _a = jnp.logical_or(_a, jnp.swapaxes(_a, -1, -2))
        _a = jnp.logical_or(_a, jnp.eye(6144, dtype=bool))
        adj = _a.astype(jnp.int32)
        return x, adj
    x, adj = _rec_inputs()
    def _L0_gnn_setup():
        import jax, jax.numpy as jnp
        import numpy as np
        N = 6144
        IN_FEATS = 512
        OUT_FEATS = 64
        NHEADS = 8
        ALPHA = 0.2
        NEG_BIG = -9000000000000000.0
        key = jax.random.key(seed)
        k_x, k_adj, k_w, k_a1, k_a2 = jax.random.split(key, 5)
        x = jax.random.normal(k_x, (N, IN_FEATS), dtype=jnp.float32)
        adj = jax.random.randint(k_adj, (N, N), 0, 2, dtype=jnp.int32)
        gain = 1.414
        bw = gain * np.sqrt(6.0 / (IN_FEATS + OUT_FEATS))
        W = jax.random.uniform(k_w, (NHEADS, IN_FEATS, OUT_FEATS), jnp.float32, -bw, bw)
        ba = gain * np.sqrt(6.0 / (OUT_FEATS + 1))
        a1 = jax.random.uniform(k_a1, (NHEADS, OUT_FEATS), jnp.float32, -ba, ba)
        a2 = jax.random.uniform(k_a2, (NHEADS, OUT_FEATS), jnp.float32, -ba, ba)
        return {'x': x, 'adj': adj, 'W': W, 'a1': a1, 'a2': a2}
    _L0_gnn_all = _L0_gnn_setup()
    _L0_gnn_in = {k: v for k, v in _L0_gnn_all.items() if k in ('W', 'a1', 'a2', )}
    del _L0_gnn_all

    return {
        "x": x,
        "adj": adj,
        "L0_gnn_W": _L0_gnn_in["W"],
        "L0_gnn_a1": _L0_gnn_in["a1"],
        "L0_gnn_a2": _L0_gnn_in["a2"],
    }

def reference(x, adj, L0_gnn_W, L0_gnn_a1, L0_gnn_a2):
    import jax
    import jax.numpy as jnp
    def _L0_gnn_ref(x, adj, W, a1, a2):
        import jax, jax.numpy as jnp
        import numpy as np
        N = 6144
        IN_FEATS = 512
        OUT_FEATS = 64
        NHEADS = 8
        ALPHA = 0.2
        NEG_BIG = -9000000000000000.0
        h = jnp.einsum('ni,hif->hnf', x, W)
        s1 = jnp.einsum('hnf,hf->hn', h, a1)
        s2 = jnp.einsum('hnf,hf->hn', h, a2)
        scores = jax.nn.leaky_relu(s1[:, :, None] + s2[:, None, :], negative_slope=ALPHA)
        scores = jnp.where(adj[None] > 0, scores, NEG_BIG)
        att = jax.nn.softmax(scores, axis=-1)
        out = jnp.einsum('hnm,hmf->hnf', att, h)
        out = jnp.transpose(out, (1, 0, 2)).reshape(N, NHEADS * OUT_FEATS)
        return jax.nn.elu(out)

    h = jnp.maximum(_layernorm(x, axis=-1), 0.0)
    x = x + _L0_gnn_ref(h, adj, L0_gnn_W, L0_gnn_a1, L0_gnn_a2)
    return x


_drawn_inputs = setup_inputs


def setup_inputs(seed=0):
    import zlib

    import numpy as np

    out = dict(_drawn_inputs(seed))
    spreads = {}
    factors = {}
    for name, (base, spread) in spreads.items():
        noise = np.random.default_rng([zlib.crc32(name.encode()), seed]).standard_normal(out[name].shape)
        drawn = base * np.exp(spread * noise) if base else spread * noise
        out[name] = jnp.asarray(drawn.astype(out[name].dtype))
    for name, factor in factors.items():
        out[name] = (out[name] * factor).astype(out[name].dtype)
    return out
```

```python
from contextlib import ExitStack

import concourse.bass as bass
from concourse import mybir

ALU = mybir.AluOpType
ACT = mybir.ActivationFunctionType
AX_X = mybir.AxisListType.X
BF16 = mybir.dt.bfloat16
F16 = mybir.dt.float16
F32 = mybir.dt.float32
I32 = mybir.dt.int32
U32 = mybir.dt.uint32

P = 128
SLOTS = 24
CHUNKS = 10
LAYERS = 3
ALPHA = 0.2
EPS = 1e-5
TINY = 1e-20
BIG = 3e38
EXP_LSB = 23
EXP_MASK = 0x7F800000


def gat_preln_kernel(nc, x, adj, W, a1, a2, out):
    N, D = x.shape
    H, _, F = W.shape
    T = N // P
    KT = D // P
    HF = H * F
    WORDS = 512
    SLICES = N // WORDS
    EDGES = CHUNKS * P
    ROW = HF + H
    XW = SLOTS + H + 1
    GROUP = 3
    BANKS = -(-CHUNKS // GROUP)
    EXPW = P + XW
    assert N % (2 * P) == 0 and D % P == 0 and HF == 512 and SLICES * WORDS == N and GROUP * EXPW <= 512

    table = nc.dram_tensor("node_table", [N, ROW], F32, kind="Internal").ap()
    w_view = W.rearrange("h (k p) f -> p k h f", p=P)

    with ExitStack() as ctx:
        def sb(name, shape, dt):
            return ctx.enter_context(nc.sbuf_tensor(name, shape, dt))

        def sem(name):
            return ctx.enter_context(nc.semaphore(name))

        bank = [ctx.enter_context(nc.psum_tensor(f"bank{i}", [P, 512], F32)) for i in range(8)]
        words_ps, turned_ps, h_ps, s_ps = bank[0:2], bank[2:4], bank[4:6], bank[6:8]
        expand_ps, acc_ps, den_ps = bank[0:4], bank[4:6], bank[6:8]

        ident = sb("ident", [P, P], F32)
        ident_b = sb("ident_b", [P, P], BF16)
        weigh = sb("weigh", [P, SLICES, P], BF16)
        before = sb("before", [P, P], BF16)
        ones_f = sb("ones_f", [P, P], F32)
        ones2 = sb("ones2", [2, P], BF16)
        low_bits = sb("low_bits", [2, WORDS], F32)
        high_bit = sb("high_bit", [2, WORDS], F32)
        column = sb("column", [2, WORDS], BF16)
        edge_no = sb("edge_no", [P, EDGES], F16)
        edge_less_slot = sb("edge_less_slot", [P, CHUNKS, SLOTS], F32)
        w_sb = sb("w_sb", [P, KT, H, F], F32)
        a_sb = sb("a_sb", [P, 2, HF], F32)
        wa = sb("wa", [P, KT, 2 * H], F32)
        eps = sb("eps", [P, 1], F32)
        minus1 = sb("minus1", [P, 1], F32)

        adj_sb = sb("adj_sb", [P, 2, N], I32)
        mask = sb("mask", [P, 2, N], BF16)
        gath = [adj_sb[:, b, 0:CHUNKS * ROW].bitcast(F32).rearrange("p (c w) -> p c w", c=CHUNKS) for b in range(2)]
        row_of = [mask[:, b, 0:2 * CHUNKS * EXPW].bitcast(F32).rearrange("p (c w) -> p c w", c=CHUNKS) for b in range(2)]
        pick = [mask[:, b, 2 * CHUNKS * EXPW:2 * CHUNKS * EXPW + EDGES] for b in range(2)]
        prep_a = adj_sb[:, 0, 0:T * (SLOTS + 1)]
        prep_b = adj_sb[:, 1, 0:T * (SLOTS + 1)]

        class dense:
            pass
        taken = [0, 0]

        def dense_tensor(b, *shape):
            n = int(shape[0] if len(shape) == 1 else shape[0] * shape[1])
            at = adj_sb[:, b, taken[b]:taken[b] + n]
            taken[b] += n
            at = at.bitcast(F32)
            return at if len(shape) == 1 else at.rearrange("p (h m) -> p h m", m=shape[1])

        dense.diag, dense.a, dense.b = (dense_tensor(0, H, P) for _ in range(3))
        dense.mask, dense.barred = dense_tensor(0, P), dense_tensor(0, P)
        dense.acc, dense.nodes = dense_tensor(0, HF), dense_tensor(0, ROW)
        dense.x, dense.out, dense.att, dense.neg_att, dense.exp_att = (dense_tensor(1, HF) for _ in range(5))
        dense.top, dense.den, dense.part, dense.s1, dense.most = (dense_tensor(1, H) for _ in range(5))
        dense.alone, dense.adj = dense_tensor(1, 1), dense_tensor(1, P).bitcast(I32)

        x_sb = sb("x_sb", [P, 2, D], F32)
        stats = sb("stats", [P, 2, 6], F32)
        mean_var = sb("mean_var", [P, 2, 2], F32)
        std = sb("std", [P, 2, 1], F32)
        rstd = sb("rstd", [P, 2, 1], F32)
        shift = sb("shift", [P, 2, 1], F32)
        hn = sb("hn", [P, 2, D], F32)
        hn_t = sb("hn_t", [P, 2, D], F32)
        row_sb = sb("row_sb", [P, 2, ROW], F32)
        s2_top = sb("s2_top", [P, H], F32)
        left1 = sb("left1", [P, WORDS], F32)
        left2 = sb("left2", [P, WORDS], F32)
        keys = sb("keys", [P, SLOTS], F32)
        keys_i = sb("keys_i", [P, SLOTS], I32)
        col_i = sb("col_i", [P, SLOTS], I32)
        col_f = sb("col_f", [P, SLOTS], F32)
        high = sb("high", [P, LAYERS, SLOTS], F32)
        rest = sb("rest", [P, LAYERS, SLOTS], F32)
        expo = sb("expo", [P, LAYERS * SLOTS], I32)
        cand = sb("cand", [P, LAYERS * SLOTS], F32)
        cand1 = sb("cand1", [P, LAYERS * SLOTS], F32)
        cand2 = sb("cand2", [P, LAYERS * SLOTS], F32)
        list_sb = sb("list_sb", [P, SLOTS], F32)

        lists = sb("lists", [P, T, SLOTS + 1], F32)
        s1_all = sb("s1_all", [P, T, H], F32)
        adj_sum = sb("adj_sum", [P, T], F32)
        degree = sb("degree", [P, T], F32)
        degree_b = sb("degree_b", [P, T], BF16)
        first_edge = sb("first_edge", [P, T], F32)
        neg_middle = sb("neg_middle", [P, T], F32)
        reach = sb("reach", [P, T], F32)
        part = [sb(f"part{i}", [P, T, XW], BF16) for i in range(2)]
        part2 = sb("part2", [P, T, H], BF16)
        resid = sb("resid", [P, T, H], F32)
        ok = sb("ok", [P, 4], F32)
        okays = sb("okays", [P, T], F32)
        den_ok = sb("den_ok", [P, T, H], F32)
        s2_max1 = sb("s2_max1", [H, 1], F32)
        s2_diag = sb("s2_diag", [H, H], F32)
        s2_max = sb("s2_max", [P, H], F32)
        verdict = sb("verdict", [P, 1], I32)

        off = sb("off", [P, 2, EDGES], F16)
        match = sb("match", [P, CHUNKS, SLOTS], F32)
        chosen = sb("chosen", [P, CHUNKS, SLOTS], F32)
        back = sb("back", [P, CHUNKS], F32)
        index = sb("index", [P, 2, CHUNKS], U32)
        z = sb("z", [P, CHUNKS, H], F32)
        zl = sb("zl", [P, CHUNKS, H], F32)
        zmax = sb("zmax", [P, CHUNKS, H], F32)
        zml = sb("zml", [P, CHUNKS, H], F32)
        score = sb("score", [P, 2, CHUNKS, H], F32)
        prob = sb("prob", [P, 2, CHUNKS, H], F32)
        den = sb("den", [P, H], F32)
        rden = sb("rden", [P, H], F32)
        att = sb("att", [P, 2, HF], F32)
        exp_att = sb("exp_att", [P, 2, HF], F32)
        res = sb("res", [P, 2, HF], F32)
        res1 = sb("res1", [P, HF], F32)
        out_sb = sb("out_sb", [P, 2, HF], F32)

        pool_const, dve_const = sem("pool_const"), sem("dve_const")
        w_landed, a1_landed, a2_landed = sem("w_landed"), sem("a1_landed"), sem("a2_landed")
        adj_landed = [sem(f"adj_landed{b}") for b in range(2)]
        x_landed = [sem(f"x_landed{b}") for b in range(2)]
        row_stored = [sem(f"row_stored{b}") for b in range(2)]
        mask_done, words_packed, words_read = sem("mask_done"), sem("words_packed"), sem("words_read")
        var_done, std_done, shift_done, hn_done = sem("var_done"), sem("std_done"), sem("shift_done"), sem("hn_done")
        hn_turned, hn_t_done, h_done = sem("hn_turned"), sem("hn_t_done"), sem("h_done")
        h_copied, s_copied = sem("h_copied"), sem("s_copied")
        listed = sem("listed")
        step = sem("step")
        prep_step, prep_pe, prep_ready = sem("prep_step"), sem("prep_pe"), sem("prep_ready")
        gath_zeroed, gather_begun = sem("gath_zeroed"), sem("gather_begun")
        off_done, pick_done, expanded, row_of_done, index_done = (
            sem("off_done"), sem("pick_done"), sem("expanded"), sem("row_of_done"), sem("index_done"))
        gathered = [sem(f"gathered{b}") for b in range(2)]
        score_done, prob_done, weighted, act_weighted, aggregated = (
            sem("score_done"), sem("prob_done"), sem("weighted"), sem("act_weighted"), sem("aggregated"))
        x2_landed = [sem(f"x2_landed{b}") for b in range(2)]
        att_done, exp_done, res_done, out_done = sem("att_done"), sem("exp_done"), sem("res_done"), sem("out_done")
        out_stored = [sem(f"out_stored{b}") for b in range(2)]
        verdict_step, verdict_pe = sem("verdict_step"), sem("verdict_pe")
        dense_free, dense_tile, dense_landed, dense_x_landed, dense_stored = (
            sem("dense_free"), sem("dense_tile"), sem("dense_landed"), sem("dense_x_landed"), sem("dense_stored"))
        dense_diag, dense_spread, dense_arg, dense_exp_done, dense_prob = (
            sem("dense_diag"), sem("dense_spread"), sem("dense_arg"), sem("dense_exp_done"), sem("dense_prob"))
        dense_begun = sem("dense_begun")
        dense_turned, dense_copied, dense_summed = sem("dense_turned"), sem("dense_copied"), sem("dense_summed")
        dense_att, dense_elu, dense_out_done = sem("dense_att"), sem("dense_elu"), sem("dense_out_done")

        MULT_DVE = 8
        DVE_PARTS = ((0, 4), (4, MULT_DVE))
        LOG_WORDS = WORDS.bit_length() - 1
        DEGREE_READY, DIAG_READY = 3, 25

        def rows(ap, t):
            return ap[bass.ts(t, P), :]

        def each_tile(eng, step, lags, first=2):
            for t in range(first):
                step(t // 2, t % 2, lambda k: 0 <= t - k < T)
            with eng.Fori(first // 2, T // 2 - 1) as i:
                for b in range(2):
                    step(i, b, lambda k: True)
            for t in range(T - 2, T + lags):
                step(t // 2, t % 2, lambda k: 0 <= t - k < T)

        def landed(i, b, lag, each=16):
            return each * (i + (b - lag) // 2 + 1)

        block = ctx.enter_context(nc.Block())

        def must_go_dense(eng):
            eng.wait_ge(verdict_step, 3)
            for b in range(2):
                eng.wait_ge(out_stored[b], 16 * (T // 2))
            return eng.value_load(verdict[0:1, 0:1], min_val=0, max_val=P) < P

        def all_visits(eng, before_tile, visit, between, after_tile):
            with eng.Fori(0, T) as t:
                before_tile(t)
                with eng.Fori(0, T) as c:
                    visit(t * (2 * T) + c, t, 0, c)
                between(t)
                with eng.Fori(0, T) as c:
                    visit(t * (2 * T) + c + T, t, 1, c)
                after_tile(t)

        def nothing(t):
            pass

        @block.sync
        def _(sp):
            for k in range(KT):
                sp.dma_start(w_sb[:, k], w_view[:, k]).then_inc(w_landed, 16)
            sp.dma_start(a_sb[:, 0, :], a1.rearrange("h f -> (h f)").partition_broadcast(P)).then_inc(a1_landed, 16)
            sp.dma_start(a_sb[:, 1, :], a2.rearrange("h f -> (h f)").partition_broadcast(P)).then_inc(a2_landed, 16)

            def load(i, b, has):
                t = 2 * i + b
                if has(2):
                    sp.wait_ge(hn_done, t - 1)
                sp.dma_start(x_sb[:, b, :], rows(x, t)).then_inc(x_landed[b], 16)
                if has(2):
                    sp.wait_ge(mask_done, t - 1)
                sp.dma_start(adj_sb[:, b, :], rows(adj, t)).then_inc(adj_landed[b], 16)
            each_tile(sp, load, 0)

            sp.wait_ge(hn_done, T)

            def residual(i, b, has):
                t = 2 * i + b
                if has(0):
                    if has(2):
                        sp.wait_ge(res_done, t - 1)
                    sp.dma_start(x_sb[:, b, :], rows(x, t)).then_inc(x2_landed[b], 16)
                if has(2):
                    sp.wait_ge(out_done, t - 1)
                    sp.dma_start(rows(out, t - 2), out_sb[:, b, :]).then_inc(out_stored[b], 16)
            each_tile(sp, residual, 2)
            for b in range(2):
                sp.wait_ge(out_stored[b], 16 * (T // 2))

            def dense_x(t):
                sp.wait_ge(dense_tile, t + 1)
                sp.sem_inc(dense_begun, 1)
                sp.dma_start(dense.x, rows(x, t)).then_inc(dense_x_landed, 16)

            def dense_load(v, t, second, c):
                sp.wait_ge(dense_free, v + 1)
                sp.sem_inc(dense_begun, 1)
                sp.dma_start(dense.adj, adj[bass.ts(t, P), bass.ts(c, P)]).then_inc(dense_landed, 16)
                sp.dma_start(dense.nodes, rows(table, c)).then_inc(dense_landed, 16)

            def dense_store(t):
                sp.wait_ge(dense_out_done, t + 1)
                sp.sem_inc(dense_begun, 1)
                sp.dma_start(rows(out, t), dense.out).then_inc(dense_stored, 16)
                sp.wait_ge(dense_stored, (t + 1) * 16)
                sp.sem_inc(dense_begun, 1)

            with sp.If(must_go_dense(sp)):
                all_visits(sp, dense_x, dense_load, nothing, dense_store)

        @block.gpsimd
        def _(pool):
            nc.gpsimd.memset(ones_f[:], 1.0).then_inc(pool_const, 1)
            nc.gpsimd.memset(ones2[:], 1.0).then_inc(pool_const, 1)
            nc.gpsimd.memset(eps[:], EPS).then_inc(pool_const, 1)
            nc.gpsimd.memset(minus1[:], -1.0).then_inc(pool_const, 1)
            nc.gpsimd.memset(s2_top[:], -BIG).then_inc(pool_const, 1)
            nc.gpsimd.iota(low_bits[:], [[0, WORDS // 256], [-1, 256]], base=255, channel_multiplier=0,
                           allow_small_or_imprecise_dtypes=True).then_inc(pool_const, 1)
            nc.gpsimd.iota(high_bit[:], [[-256, WORDS // 256], [0, 256]], base=WORDS - 256, channel_multiplier=0,
                           allow_small_or_imprecise_dtypes=True).then_inc(pool_const, 1)
            nc.gpsimd.iota(edge_no[:], [[1, EDGES]], base=0, channel_multiplier=0,
                           allow_small_or_imprecise_dtypes=True).then_inc(pool_const, 1)
            nc.gpsimd.iota(edge_less_slot[:], [[P, CHUNKS], [-1, SLOTS]], base=0, channel_multiplier=1,
                           allow_small_or_imprecise_dtypes=True).then_inc(pool_const, 1)
            pool.wait_ge(pool_const, 9)
            nc.gpsimd.affine_select(out=ident[:], in_=ones_f[:], compare_op=ALU.is_equal, fill=0.0, base=0,
                                    pattern=[[-1, P]], channel_multiplier=1).then_inc(pool_const, 1)
            nc.gpsimd.affine_select(out=before[:], in_=ones_f[:], compare_op=ALU.is_gt, fill=0.0, base=0,
                                    pattern=[[1, P]], channel_multiplier=-1).then_inc(pool_const, 1)

            def store_row(i, b, has):
                t = 2 * i + b
                if has(1):
                    pool.wait_ge(h_copied, t)
                    pool.wait_ge(s_copied, t)
                    pool.dma_start(rows(table, t - 1), row_sb[:, 1 - b, :]).then_inc(row_stored[1 - b], 16)
            each_tile(pool, store_row, 1)

            pool.wait_ge(prep_ready, 1)
            for b in range(2):
                nc.gpsimd.memset(gath[b], 0.0).then_inc(gath_zeroed, 1)
            pool.wait_ge(gath_zeroed, 2)
            for b in range(2):
                pool.wait_ge(row_stored[b], 16 * (T // 2))

            def gather(i, b, has):
                t = 2 * i + b
                pool.wait_ge(index_done, t + 1)
                if has(2):
                    pool.wait_ge(aggregated, t - 1)
                pool.sem_inc(gather_begun, 1)
                for c in range(CHUNKS):
                    nc.gpsimd.indirect_dma_start(
                        gath[b][:, c, :], None, table, bass.IndirectOffsetOnAxis(index[:, b, c:c + 1], 0),
                        bounds_check=N - 1, oob_is_err=False).then_inc(gathered[b], 16)
            each_tile(pool, gather, 0)

        @block.scalar
        def _(act):
            def node_step(i, b, has):
                t = 2 * i + b
                if has(0):
                    act.wait_ge(adj_landed[b], landed(i, b, 0))
                    if has(2):
                        act.wait_ge(words_packed, t - 1)
                    nc.scalar.activation(mask[:, b, :], adj_sb[:, b, :], ACT.Relu,
                                         accum_out=adj_sum[:, bass.ds(t, 1)]).then_inc(mask_done, 1)
                    act.wait_ge(shift_done, t + 1)
                    if has(2):
                        act.wait_ge(hn_turned, t - 1)
                    nc.scalar.activation(hn[:, b, :], x_sb[:, b, :], ACT.Relu, scale=rstd[:, b, :],
                                         bias=shift[:, b, :]).then_inc(hn_done, 1)
                if has(-1):
                    act.wait_ge(var_done, t + 2)
                    nc.scalar.activation(std[:, 1 - b, :], mean_var[:, 1 - b, 1:2], ACT.Sqrt,
                                         bias=eps[:]).then_inc(std_done, 1)
                if has(1):
                    act.wait_ge(h_done, t)
                    if has(3):
                        act.wait_ge(row_stored[1 - b], landed(i, b, 3))
                    nc.scalar.copy(row_sb[:, 1 - b, 0:HF], h_ps[1 - b][:]).then_inc(h_copied, 1)

            act.wait_ge(pool_const, 11)
            act.wait_ge(var_done, 1)
            nc.scalar.activation(std[:, 0, :], mean_var[:, 0, 1:2], ACT.Sqrt, bias=eps[:]).then_inc(std_done, 1)
            each_tile(act, node_step, 1, first=4)

            def distances(i, b, has, lag):
                t = 2 * i + b - lag
                if has(2 + lag):
                    act.wait_ge(pick_done, t - 1)
                nc.scalar.activation(off[:, (b - lag) % 2, :], edge_no[:], ACT.Abs,
                                     bias=neg_middle[:, bass.ds(t, 1)]).then_inc(off_done, 1)

            act.wait_ge(prep_ready, 1)
            distances(0, 0, lambda k: k == 0, 0)

            def edge_step(i, b, has):
                t = 2 * i + b
                if has(0):
                    act.wait_ge(expanded, t + 1)
                    if has(2):
                        act.wait_ge(aggregated, t - 1)
                    for g in range(BANKS):
                        n = min(GROUP, CHUNKS - g * GROUP)
                        last = nc.scalar.copy(row_of[b][:, g * GROUP:g * GROUP + n, :],
                                              expand_ps[g][:, 0:n * EXPW].rearrange("p (c w) -> p c w", w=EXPW))
                    last.then_inc(row_of_done, 1)
                if has(-1):
                    distances(i, b, has, -1)
                if has(1):
                    act.wait_ge(score_done, t)
                    if has(3):
                        act.wait_ge(aggregated, t - 2)
                    nc.scalar.activation(prob[:, 1 - b], score[:, 1 - b], ACT.Exp).then_inc(prob_done, 1)
                    act.wait_ge(prob_done, t)
                    act.wait_ge(gathered[1 - b], landed(i, b, 1, 16 * CHUNKS))
                    for c in range(MULT_DVE, CHUNKS):
                        for h in range(H):
                            piece = gath[1 - b][:, c, h * F:(h + 1) * F]
                            last = nc.scalar.mul(piece, piece, prob[:, 1 - b, c, h:h + 1])
                        last.then_inc(act_weighted, 1)
                if has(2):
                    act.wait_ge(att_done, t - 1)
                    if has(4):
                        act.wait_ge(res_done, t - 3)
                    nc.scalar.activation(exp_att[:, b, :], att[:, b, :], ACT.Exp).then_inc(exp_done, 1)
                if has(3):
                    act.wait_ge(res_done, t - 2)
                    if has(5):
                        act.wait_ge(out_stored[1 - b], landed(i, b, 5))
                    nc.scalar.activation(out_sb[:, 1 - b, :], res[:, 1 - b, :], ACT.Identity,
                                         bias=minus1[:]).then_inc(out_done, 1)
            each_tile(act, edge_step, 3, first=6)

            def dense_exp(v, t, second, c):
                if second:
                    act.wait_ge(dense_arg, t * T + c + 1)
                    nc.scalar.activation(dense.b, dense.b, ACT.Exp).then_inc(dense_exp_done, 1)

            def dense_elu_exp(t):
                act.wait_ge(dense_att, t + 1)
                nc.scalar.activation(dense.exp_att, dense.neg_att, ACT.Exp).then_inc(dense_elu, 1)

            with act.If(must_go_dense(act)):
                all_visits(act, nothing, dense_exp, nothing, dense_elu_exp)

        @block.vector
        def _(dve):
            dve.wait_ge(pool_const, 11)
            nc.vector.tensor_copy(ident_b[:], ident[:]).then_inc(dve_const, 1)
            for j in range(SLICES):
                nc.vector.tensor_scalar(weigh[:, j, :], ident[:], float(WORDS << (SLICES - 1 - j)), None,
                                        ALU.mult).then_inc(dve_const, 1)
            nc.vector.tensor_scalar(low_bits[:], low_bits[:], ident[0:2, 0:1], None, ALU.mult).then_inc(dve_const, 1)
            dve.wait_ge(dve_const, SLICES + 2)
            nc.vector.scalar_tensor_tensor(out=column[:], in0=high_bit[:], scalar=ident[0:2, 1:2], in1=low_bits[:],
                                           op0=ALU.mult, op1=ALU.add).then_inc(dve_const, 1)
            dve.wait_ge(w_landed, 16 * KT)
            dve.wait_ge(a1_landed, 16)
            dve.wait_ge(a2_landed, 16)
            done = SLICES + 3
            for k in range(KT):
                for s in range(2):
                    scratch = hn[:, s, :]
                    nc.vector.tensor_tensor(scratch, w_sb[:, k].rearrange("p h f -> p (h f)"), a_sb[:, s, :],
                                            ALU.mult).then_inc(dve_const, 1)
                    dve.wait_ge(dve_const, done + 1)
                    nc.vector.tensor_reduce(wa[:, k, s * H:(s + 1) * H], scratch.rearrange("p (h f) -> p h f", h=H),
                                            AX_X, ALU.add).then_inc(dve_const, 1)
                    dve.wait_ge(dve_const, done + 2)
                    done += 2

            def settle(n):
                dve.wait_ge(step, n)
                dve.sem_clear(step)

            def statistics(b, i_landed):
                dve.wait_ge(x_landed[b], i_landed)
                nc.vector.bn_stats(stats[:, b, :], x_sb[:, b, :]).then_inc(step, 1)
                settle(1)
                nc.vector.bn_aggr(mean_var[:, b, :], stats[:, b, :]).then_inc(var_done, 1)

            def extract(t, words):
                nc.vector.max(keys[:, 0:8], words[:]).then_inc(step, 1)
                dve.wait_ge(step, 1)
                nc.vector.match_replace(left1[:], keys[:, 0:8], words[:], 0.0).then_inc(step, 1)
                dve.wait_ge(step, 2)
                dve.sem_inc(words_read, 1)
                nc.vector.max(keys[:, 8:16], left1[:]).then_inc(step, 1)
                dve.wait_ge(step, 3)
                nc.vector.match_replace(left2[:], keys[:, 8:16], left1[:], 0.0).then_inc(step, 1)
                dve.wait_ge(step, 4)
                nc.vector.max(keys[:, 16:24], left2[:]).then_inc(step, 1)
                dve.wait_ge(step, 5)
                exp_bits = lambda ap: ap.bitcast(I32)
                nc.vector.tensor_scalar(exp_bits(high[:, 0, :]), exp_bits(keys[:]), EXP_MASK, None,
                                        ALU.bitwise_and).then_inc(step, 1)
                nc.vector.tensor_copy(keys_i[:], keys[:]).then_inc(step, 1)
                dve.wait_ge(step, 7)
                nc.vector.tensor_tensor(rest[:, 1, :], keys[:], high[:, 0, :], ALU.subtract).then_inc(step, 1)
                nc.vector.tensor_scalar(col_i[:], keys_i[:], WORDS - 1, None, ALU.bitwise_and).then_inc(step, 1)
                dve.wait_ge(step, 9)
                nc.vector.tensor_scalar(exp_bits(high[:, 1, :]), exp_bits(rest[:, 1, :]), EXP_MASK, None,
                                        ALU.bitwise_and).then_inc(step, 1)
                nc.vector.tensor_scalar(col_f[:], col_i[:], float(1 - WORDS * (127 + LOG_WORDS)), None,
                                        ALU.add).then_inc(step, 1)
                dve.wait_ge(step, 11)
                nc.vector.tensor_tensor(rest[:, 2, :], rest[:, 1, :], high[:, 1, :],
                                        ALU.subtract).then_inc(step, 1)
                dve.wait_ge(step, 12)
                nc.vector.tensor_scalar(exp_bits(high[:, 2, :]), exp_bits(rest[:, 2, :]), EXP_MASK, None,
                                        ALU.bitwise_and).then_inc(step, 1)
                dve.wait_ge(step, 13)
                nc.vector.tensor_scalar(expo[:], exp_bits(high[:].rearrange("p l s -> p (l s)")), EXP_LSB, None,
                                        ALU.logical_shift_right).then_inc(step, 1)
                dve.wait_ge(step, 14)
                nc.vector.scalar_tensor_tensor(
                    out=cand[:].rearrange("p (l s) -> p l s", l=LAYERS), in0=expo[:].rearrange("p (l s) -> p l s", l=LAYERS),
                    scalar=float(WORDS), in1=col_f[:, None, :].broadcast_to([P, LAYERS, SLOTS]),
                    op0=ALU.mult, op1=ALU.add).then_inc(step, 1)
                dve.wait_ge(step, 15)
                nc.vector.max(list_sb[:, 0:8], cand[:]).then_inc(step, 1)
                dve.wait_ge(step, 16)
                nc.vector.match_replace(cand1[:], list_sb[:, 0:8], cand[:], -BIG).then_inc(step, 1)
                dve.wait_ge(step, 17)
                nc.vector.max(list_sb[:, 8:16], cand1[:]).then_inc(step, 1)
                dve.wait_ge(step, 18)
                nc.vector.match_replace(cand2[:], list_sb[:, 8:16], cand1[:], -BIG).then_inc(step, 1)
                dve.wait_ge(step, 19)
                nc.vector.max(list_sb[:, 16:24], cand2[:]).then_inc(step, 1)
                settle(20)
                nc.vector.tensor_scalar(lists[:, bass.ds(t, 1), 0:SLOTS], list_sb[:, None, :], 0.0, None,
                                        ALU.max).then_inc(listed, 1)


            def node_step(i, b, has):
                t = 2 * i + b
                if has(0):
                    dve.wait_ge(std_done, t + 1)
                    if has(2):
                        dve.wait_ge(hn_done, t - 1)
                    nc.vector.reciprocal(rstd[:, b, :], std[:, b, :]).then_inc(step, 1)
                    settle(1)
                    nc.vector.scalar_tensor_tensor(out=shift[:, b, :], in0=mean_var[:, b, 0:1], scalar=-1.0,
                                                   in1=rstd[:, b, :], op0=ALU.mult, op1=ALU.mult).then_inc(shift_done, 1)
                if has(-1):
                    statistics(1 - b, landed(i, b, -1))
                if has(1):
                    dve.wait_ge(words_packed, t)
                    dve.wait_ge(h_done, t)
                    if has(3):
                        dve.wait_ge(row_stored[1 - b], landed(i, b, 3))
                    nc.vector.tensor_copy(row_sb[:, 1 - b, HF:ROW], s_ps[1 - b][:, H:2 * H])
                    nc.vector.tensor_copy(s1_all[:, bass.ds(t - 1, 1), :], s_ps[1 - b][:, None, 0:H])
                    if has(2):
                        dve.wait_ge(s_copied, t - 1)
                    nc.vector.tensor_tensor(s2_top[:], s_ps[1 - b][:, H:2 * H], s2_top[:], ALU.max).then_inc(s_copied, 1)
                    extract(t - 1, words_ps[1 - b])
                if has(0):
                    dve.wait_ge(hn_turned, t + 1)
                    if has(2):
                        dve.wait_ge(h_done, t - 1)
                    nc.vector.tensor_copy(hn_t[:, b, :], turned_ps[b][:]).then_inc(hn_t_done, 1)

            statistics(0, 16)
            each_tile(dve, node_step, 1, first=4)

            prepped = [0]

            def link(instruction):
                prepped[0] += 1
                instruction.then_inc(prep_step, 1)
                dve.wait_ge(prep_step, prepped[0])

            every = lambda ap: ap.rearrange("p (t s) -> p t s", t=T)
            whole, low_part = every(prep_a), every(prep_b)
            dve.wait_ge(listed, T)
            dve.wait_ge(mask_done, T)
            dve.wait_ge(s_copied, T)
            positive = whole[:, :, 0:SLOTS].bitcast(F32)
            link(nc.vector.tensor_scalar(positive, lists[:, :, 0:SLOTS], 0.0, None, ALU.is_gt))
            link(nc.vector.tensor_reduce(degree[:], positive, AX_X, ALU.add))
            link(nc.vector.tensor_copy(degree_b[:], degree[:]))
            degree_ready = prepped[0]
            dve.wait_ge(prep_pe, 2)
            link(nc.vector.tensor_copy(lists[:, :, SLOTS], words_ps[0][:, 0:T]))
            link(nc.vector.tensor_copy(first_edge[:], words_ps[0][:, 0:T]))
            link(nc.vector.scalar_tensor_tensor(out=neg_middle[:], in0=degree[:], scalar=-0.5, in1=first_edge[:],
                                                op0=ALU.mult, op1=ALU.subtract))
            link(nc.vector.tensor_scalar(neg_middle[:], neg_middle[:], 0.5, None, ALU.add))
            link(nc.vector.tensor_scalar(reach[:], degree[:], 0.5, -0.25, ALU.mult, ALU.add))
            link(nc.vector.tensor_tensor(okays[:], degree[:], adj_sum[:], ALU.is_equal))
            link(nc.vector.tensor_reduce(ok[:, 0:1], okays[:], AX_X, ALU.min))
            link(nc.vector.tensor_tensor(okays[:], degree[:], first_edge[:], ALU.add))
            link(nc.vector.tensor_scalar(okays[:], okays[:], float(EDGES), None, ALU.is_le))
            link(nc.vector.tensor_reduce(ok[:, 1:2], okays[:], AX_X, ALU.min))
            link(nc.vector.tensor_copy(whole, lists[:]))
            link(nc.vector.tensor_scalar(low_part, whole, 63, None, ALU.bitwise_and))
            link(nc.vector.tensor_copy(part[1][:, :, 0:SLOTS + 1], low_part))
            link(nc.vector.tensor_scalar(whole, whole, ~63, None, ALU.bitwise_and))
            link(nc.vector.tensor_copy(part[0][:, :, 0:SLOTS + 1], whole))
            link(nc.vector.tensor_copy(part[0][:, :, SLOTS + 1:XW], s1_all[:]))
            link(nc.vector.tensor_tensor(resid[:], s1_all[:], part[0][:, :, SLOTS + 1:XW], ALU.subtract))
            link(nc.vector.tensor_copy(part[1][:, :, SLOTS + 1:XW], resid[:]))
            link(nc.vector.tensor_tensor(resid[:], resid[:], part[1][:, :, SLOTS + 1:XW], ALU.subtract))
            link(nc.vector.tensor_copy(part2[:], resid[:]))
            link(nc.vector.tensor_reduce(s2_max1[:], words_ps[1][0:H, 0:P], AX_X, ALU.max))
            link(nc.vector.tensor_scalar(s2_diag[:], ident[0:H, 0:H], s2_max1[:], None, ALU.mult))
            diag_ready = prepped[0]
            dve.wait_ge(prep_pe, 3)
            nc.vector.tensor_copy(s2_max[:], turned_ps[0][:, 0:H]).then_inc(prep_ready, 1)
            assert (degree_ready, diag_ready) == (DEGREE_READY, DIAG_READY), (degree_ready, diag_ready)

            def choose(i, b, has, lag):
                t = 2 * i + b - lag
                dve.wait_ge(off_done, t + 1)
                if has(2 + lag):
                    dve.wait_ge(expanded, t - 1)
                nc.vector.tensor_scalar(pick[(b - lag) % 2], off[:, (b - lag) % 2, :], reach[:, bass.ds(t, 1)], None,
                                        ALU.is_le).then_inc(pick_done, 1)

            def edge_step(i, b, has):
                t = 2 * i + b
                if has(0):
                    dve.wait_ge(row_of_done, t + 1)
                    nc.vector.tensor_tensor(match[:], edge_less_slot[:],
                                            row_of[b][:, :, P + SLOTS:P + SLOTS + 1].broadcast_to([P, CHUNKS, SLOTS]),
                                            ALU.is_equal).then_inc(step, 1)
                    dve.wait_ge(step, 1)
                    nc.vector.tensor_tensor(chosen[:], match[:], row_of[b][:, :, P:P + SLOTS],
                                            ALU.mult).then_inc(step, 1)
                    dve.wait_ge(step, 2)
                    nc.vector.tensor_reduce(back[:], chosen[:], AX_X, ALU.add).then_inc(step, 1)
                    settle(3)
                    if has(2):
                        dve.wait_ge(gathered[b], landed(i, b, 2, 16 * CHUNKS))
                    nc.vector.tensor_scalar(index[:, b, :], back[:], -1.0, float(N), ALU.mult,
                                            ALU.add).then_inc(index_done, 1)
                if has(1):
                    dve.wait_ge(gathered[1 - b], landed(i, b, 1, 16 * CHUNKS))
                    s1_e = row_of[1 - b][:, :, P + SLOTS + 1:EXPW]
                    nc.vector.tensor_tensor(z[:], s1_e, gath[1 - b][:, :, HF:ROW], ALU.add).then_inc(step, 1)
                    nc.vector.tensor_tensor(zmax[:], s1_e, s2_max[:, None, :].broadcast_to([P, CHUNKS, H]),
                                            ALU.add).then_inc(step, 1)
                    dve.wait_ge(step, 2)
                    nc.vector.scalar_tensor_tensor(out=zl[:], in0=z[:], scalar=ALPHA, in1=z[:], op0=ALU.mult,
                                                   op1=ALU.max).then_inc(step, 1)
                    nc.vector.scalar_tensor_tensor(out=zml[:], in0=zmax[:], scalar=ALPHA, in1=zmax[:], op0=ALU.mult,
                                                   op1=ALU.max).then_inc(step, 1)
                    settle(4)
                    if has(3):
                        dve.wait_ge(prob_done, t - 2)
                    nc.vector.tensor_tensor(score[:, 1 - b], zl[:], zml[:], ALU.subtract).then_inc(score_done, 1)
                if has(-1):
                    choose(i, b, has, -1)
                if has(2):
                    dve.wait_ge(aggregated, t - 1)
                    nc.vector.tensor_scalar(den_ok[:, bass.ds(t - 2, 1), :], den_ps[b][:, None, 0:H], TINY, None,
                                            ALU.is_ge).then_inc(step, 1)
                    nc.vector.tensor_scalar(den[:], den_ps[b][:, 0:H], TINY, None, ALU.max).then_inc(step, 1)
                    dve.wait_ge(step, 2)
                    nc.vector.reciprocal(rden[:], den[:]).then_inc(step, 1)
                    settle(3)
                    if has(4):
                        dve.wait_ge(exp_done, t - 3)
                    nc.vector.tensor_tensor(att[:, b, :].rearrange("p (h f) -> p h f", h=H),
                                            acc_ps[b][:].rearrange("p (h f) -> p h f", h=H),
                                            rden[:, :, None].broadcast_to([P, H, F]), ALU.mult).then_inc(att_done, 1)
                if has(3):
                    dve.wait_ge(exp_done, t - 2)
                    dve.wait_ge(x2_landed[1 - b], landed(i, b, 3))
                    if has(4):
                        dve.wait_ge(res_done, t - 3)
                    nc.vector.scalar_tensor_tensor(out=res1[:], in0=exp_att[:, 1 - b, :], scalar=1.0, in1=x_sb[:, 1 - b, :],
                                                   op0=ALU.min, op1=ALU.add).then_inc(step, 1)
                    settle(1)
                    if has(5):
                        dve.wait_ge(out_done, t - 4)
                    nc.vector.scalar_tensor_tensor(out=res[:, 1 - b, :], in0=att[:, 1 - b, :], scalar=0.0, in1=res1[:],
                                                   op0=ALU.max, op1=ALU.add).then_inc(res_done, 1)
                if has(1):
                    dve.wait_ge(prob_done, t)
                    for c0, c1 in DVE_PARTS:
                        piece = gath[1 - b][:, c0:c1, 0:HF].rearrange("p c (h f) -> p c h f", h=H)
                        nc.vector.tensor_tensor(piece, piece, prob[:, 1 - b, c0:c1, :, None].broadcast_to(
                            [P, c1 - c0, H, F]), ALU.mult).then_inc(weighted, 1)

            dve.wait_ge(prep_ready, 1)
            choose(0, 0, lambda k: k == 0, 0)
            each_tile(dve, edge_step, 3, first=6)

            dve.wait_ge(att_done, T)
            nc.vector.tensor_reduce(ok[:, 2:3], den_ok[:].rearrange("p t h -> p (t h)"), AX_X,
                                    ALU.min).then_inc(verdict_step, 1)
            dve.wait_ge(verdict_step, 1)
            nc.vector.tensor_reduce(ok[:, 3:4], ok[:, 0:3], AX_X, ALU.min).then_inc(verdict_step, 1)
            dve.wait_ge(verdict_pe, 1)
            nc.vector.tensor_copy(verdict[0:1, :], expand_ps[0][0:1, 0:1]).then_inc(verdict_step, 1)

            def over_nodes(ap):
                return ap[:, :, None].broadcast_to([P, H, P])

            def over_heads(ap):
                return ap[:, None, :].broadcast_to([P, H, P])

            def alone(instruction):
                instruction.then_inc(step, 1)
                settle(1)

            def dense_start(t):
                alone(nc.vector.memset(dense.top, -BIG))
                alone(nc.vector.memset(dense.den, 0.0))
                alone(nc.vector.memset(dense.acc, 0.0))

            def dense_visit(v, t, second, c):
                dve.wait_ge(dense_landed, (v + 1) * 32)
                nc.vector.tensor_tensor(dense.diag, over_heads(ident[:]), over_nodes(dense.nodes[:, HF:ROW]),
                                        ALU.mult).then_inc(dense_diag, 1)
                alone(nc.vector.tensor_scalar(dense.mask, dense.adj, 0.0, None, ALU.is_gt))
                dve.wait_ge(dense_spread, v + 1)
                for half in range(2):
                    alone(nc.vector.tensor_copy(dense.a[:, half * (H // 2):(half + 1) * (H // 2), :],
                                                bank[half][:].rearrange("p (h m) -> p h m", m=P)))
                if not second:
                    alone(nc.vector.tensor_scalar(dense.barred, dense.mask, -1.0, BIG, ALU.add, ALU.mult))
                    alone(nc.vector.tensor_tensor(dense.b, dense.a, over_heads(dense.mask), ALU.mult))
                    alone(nc.vector.tensor_tensor(dense.b, dense.b, over_heads(dense.barred), ALU.add))
                    alone(nc.vector.tensor_reduce(dense.part, dense.b, AX_X, ALU.max))
                    nc.vector.tensor_tensor(dense.top, dense.top, dense.part, ALU.max).then_inc(dense_free, 1)
                    return
                alone(nc.vector.tensor_tensor(dense.a, dense.a, over_nodes(dense.s1), ALU.add))
                alone(nc.vector.scalar_tensor_tensor(out=dense.b, in0=dense.a, scalar=ALPHA, in1=dense.a,
                                                     op0=ALU.mult, op1=ALU.max))
                alone(nc.vector.tensor_tensor(dense.b, dense.b, over_nodes(dense.most), ALU.subtract))
                nc.vector.tensor_scalar(dense.b, dense.b, 0.0, None, ALU.min).then_inc(dense_arg, 1)
                dve.wait_ge(dense_exp_done, t * T + c + 1)
                alone(nc.vector.tensor_tensor(dense.b, dense.b, over_heads(dense.mask), ALU.mult))
                nc.vector.tensor_scalar(dense.b, dense.b, dense.alone, None, ALU.add).then_inc(dense_prob, 1)
                dve.wait_ge(dense_prob, t * T + c + 1)
                alone(nc.vector.tensor_reduce(dense.part, dense.b, AX_X, ALU.add))
                alone(nc.vector.tensor_tensor(dense.den, dense.den, dense.part, ALU.add))
                dve.wait_ge(dense_turned, t * T + c + 1)
                for half in range(2):
                    last = nc.vector.tensor_copy(dense.diag[:, half * (H // 2):(half + 1) * (H // 2), :],
                                                 bank[2 + half][:].rearrange("p (h m) -> p h m", m=P))
                last.then_inc(dense_copied, 1)
                dve.wait_ge(dense_summed, t * T + c + 1)
                nc.vector.tensor_tensor(dense.acc, dense.acc, bank[4][:], ALU.add).then_inc(dense_free, 1)

            def dense_most(t):
                dve.wait_ge(dense_free, t * (2 * T) + T + 1)
                alone(nc.vector.tensor_copy(dense.s1[:, None, :], s1_all[:, bass.ds(t, 1), :]))
                alone(nc.vector.tensor_tensor(dense.part, dense.s1, dense.top, ALU.add))
                alone(nc.vector.scalar_tensor_tensor(out=dense.most, in0=dense.part, scalar=ALPHA, in1=dense.part,
                                                     op0=ALU.mult, op1=ALU.max))
                alone(nc.vector.tensor_scalar(dense.alone, dense.top[:, 0:1], -BIG / 2, None, ALU.is_lt))

            def dense_finish(t):
                dve.wait_ge(dense_free, (t + 1) * (2 * T) + 1)
                alone(nc.vector.reciprocal(dense.part, dense.den))
                alone(nc.vector.tensor_tensor(dense.att.rearrange("p (h f) -> p h f", h=H),
                                              dense.acc.rearrange("p (h f) -> p h f", h=H),
                                              dense.part[:, :, None].broadcast_to([P, H, F]), ALU.mult))
                nc.vector.tensor_scalar(dense.neg_att, dense.att, 0.0, None, ALU.min).then_inc(dense_att, 1)
                dve.wait_ge(dense_elu, t + 1)
                alone(nc.vector.scalar_tensor_tensor(out=dense.att, in0=dense.att, scalar=0.0, in1=dense.exp_att,
                                                     op0=ALU.max, op1=ALU.add))
                dve.wait_ge(dense_x_landed, (t + 1) * 16)
                nc.vector.scalar_tensor_tensor(out=dense.out, in0=dense.att, scalar=-1.0, in1=dense.x,
                                               op0=ALU.add, op1=ALU.add).then_inc(dense_out_done, 1)
                dve.wait_ge(dense_stored, (t + 1) * 16)
                dve.sem_inc(dense_tile, 1)

            with dve.If(must_go_dense(dve)):
                dve.sem_inc(dense_free, 1)
                dve.sem_inc(dense_tile, 1)
                all_visits(dve, dense_start, dense_visit, dense_most, dense_finish)

        @block.tensor
        def _(pe):
            def node_step(i, b, has):
                t = 2 * i + b
                if has(1):
                    pe.wait_ge(hn_t_done, t)
                    if has(3):
                        pe.wait_ge(h_copied, t - 2)
                        pe.wait_ge(s_copied, t - 2)
                    for k in range(KT):
                        nc.tensor.matmul(h_ps[1 - b][:], hn_t[:, 1 - b, k * P:(k + 1) * P],
                                         w_sb[:, k].rearrange("p h f -> p (h f)"), start=(k == 0), stop=(k == KT - 1))
                        last = nc.tensor.matmul(s_ps[1 - b][:, 0:2 * H], hn_t[:, 1 - b, k * P:(k + 1) * P],
                                                wa[:, k, :], start=(k == 0), stop=(k == KT - 1))
                    last.then_inc(h_done, 1)
                if has(0):
                    pe.wait_ge(mask_done, t + 1)
                    if has(2):
                        pe.wait_ge(words_read, t - 1)
                    nc.tensor.matmul(words_ps[b][:], ones2[:], column[:], start=True, stop=False)
                    for j in range(SLICES):
                        last = nc.tensor.matmul(words_ps[b][:], weigh[:, j, :], mask[:, b, j * WORDS:(j + 1) * WORDS],
                                                start=False, stop=(j == SLICES - 1))
                    last.then_inc(words_packed, 1)
                    pe.wait_ge(hn_done, t + 1)
                    if has(2):
                        pe.wait_ge(hn_t_done, t - 1)
                    for k in range(KT):
                        last = nc.tensor.transpose(turned_ps[b][:, k * P:(k + 1) * P], hn[:, b, k * P:(k + 1) * P], ident[:])
                    last.then_inc(hn_turned, 1)

            pe.wait_ge(pool_const, 11)
            pe.wait_ge(w_landed, 16 * KT)
            pe.wait_ge(dve_const, SLICES + 3 + 4 * KT)
            each_tile(pe, node_step, 1, first=4)

            pe.wait_ge(prep_step, DEGREE_READY)
            nc.tensor.matmul(words_ps[0][:, 0:T], before[:], degree_b[:], start=True, stop=True).then_inc(prep_pe, 1)
            pe.wait_ge(s_copied, T)
            nc.tensor.transpose(words_ps[1][0:H, 0:P], s2_top[:], ident[:]).then_inc(prep_pe, 1)
            pe.wait_ge(prep_step, DIAG_READY)
            nc.tensor.matmul(turned_ps[0][:, 0:H], ones_f[0:H, :], s2_diag[:], start=True, stop=True).then_inc(prep_pe, 1)

            def expand(i, b, has, lag):
                t = 2 * i + b - lag
                pe.wait_ge(pick_done, t + 1)
                if has(1 + lag):
                    pe.wait_ge(row_of_done, t)
                for c in range(CHUNKS):
                    one_hot = pick[(b - lag) % 2][:, c * P:(c + 1) * P]
                    to = expand_ps[c // GROUP][:, (c % GROUP) * EXPW:(c % GROUP + 1) * EXPW]
                    nc.tensor.matmul(to[:, 0:P], one_hot, ident_b[:], start=True, stop=True)
                    nc.tensor.matmul(to[:, P:EXPW], one_hot, part[0][:, bass.ds(t, 1), :].rearrange("p a w -> p (a w)"),
                                     start=True, stop=False)
                    nc.tensor.matmul(to[:, P + SLOTS + 1:EXPW], one_hot,
                                     part2[:, bass.ds(t, 1), :].rearrange("p a w -> p (a w)"), start=False, stop=False)
                    last = nc.tensor.matmul(to[:, P:EXPW], one_hot,
                                            part[1][:, bass.ds(t, 1), :].rearrange("p a w -> p (a w)"),
                                            start=False, stop=True)
                last.then_inc(expanded, 1)

            def edge_step(i, b, has):
                t = 2 * i + b
                if has(-1):
                    expand(i, b, has, -1)
                if has(1):
                    if has(3):
                        pe.wait_ge(att_done, t - 2)
                    ready = [(c1, weighted, len(DVE_PARTS) * (t - 1) + n + 1) for n, (_, c1) in enumerate(DVE_PARTS)]
                    waits = {c0: ready[n] for n, (c0, _) in enumerate(DVE_PARTS)}
                    for c in range(CHUNKS):
                        if c in waits:
                            pe.wait_ge(weighted, waits[c][2])
                        if c >= MULT_DVE:
                            pe.wait_ge(act_weighted, (CHUNKS - MULT_DVE) * (t - 1) + c - MULT_DVE + 1)
                        one_hot = row_of[1 - b][:, c, 0:P]
                        nc.tensor.matmul(acc_ps[1 - b][:], one_hot, gath[1 - b][:, c, 0:HF], start=(c == 0),
                                         stop=(c == CHUNKS - 1))
                        last = nc.tensor.matmul(den_ps[1 - b][:, 0:H], one_hot, prob[:, 1 - b, c, :], start=(c == 0),
                                                stop=(c == CHUNKS - 1))
                    last.then_inc(aggregated, 1)

            pe.wait_ge(prep_ready, 1)
            expand(0, 0, lambda k: k == 0, 0)
            each_tile(pe, edge_step, 3, first=4)

            pe.wait_ge(verdict_step, 2)
            nc.tensor.matmul(expand_ps[0][0:1, 0:1], ok[:, 3:4], ones_f[:, 0:1], start=True, stop=True).then_inc(verdict_pe, 1)

            def dense_products(v, t, second, c):
                pe.wait_ge(dense_diag, v + 1)
                for half in range(2):
                    last = nc.tensor.matmul(bank[half][:], ones_f[:], dense.diag[:, half * (H // 2):(half + 1) * (H // 2), :]
                                            .rearrange("p h m -> p (h m)"), start=True, stop=True)
                last.then_inc(dense_spread, 1)
                if second:
                    pe.wait_ge(dense_prob, t * T + c + 1)
                    for h in range(H):
                        last = nc.tensor.transpose(bank[2 + h // (H // 2)][:, (h % (H // 2)) * P:(h % (H // 2) + 1) * P],
                                                   dense.b[:, h, :], ident[:])
                    last.then_inc(dense_turned, 1)
                    pe.wait_ge(dense_copied, t * T + c + 1)
                    for h in range(H):
                        last = nc.tensor.matmul(bank[4][:, h * F:(h + 1) * F], dense.diag[:, h, :],
                                                dense.nodes[:, h * F:(h + 1) * F], start=True, stop=True)
                    last.then_inc(dense_summed, 1)

            with pe.If(must_go_dense(pe)):
                all_visits(pe, nothing, dense_products, nothing, nothing)


def kernel(**inputs):
    import numpy as _np
    import concourse.bacc as _bacc
    from concourse import mybir as _mybir
    from concourse.bass_utils import run_bass_kernel_spmd as _run

    nc = _bacc.Bacc("TRN2", target_bir_lowering=False, num_devices=1)
    arrays, args = {}, []
    for name in ("x", "adj", "L0_gnn_W", "L0_gnn_a1", "L0_gnn_a2"):
        a = _np.ascontiguousarray(inputs[name])
        arrays[f"in_{name}"] = a
        args.append(nc.dram_tensor(f"in_{name}", a.shape, _mybir.dt.from_np(a.dtype), kind="ExternalInput").ap())
    out = nc.dram_tensor("out", inputs["x"].shape, _mybir.dt.float32, kind="ExternalOutput").ap()
    gat_preln_kernel(nc, *args, out)
    r = _run(nc, [arrays], core_ids=[0])
    return r.results[0]["out"]
```

```python
from contextlib import ExitStack

import concourse.bass as bass
from concourse import mybir

ALU = mybir.AluOpType
ACT = mybir.ActivationFunctionType
AX_X = mybir.AxisListType.X
BF16 = mybir.dt.bfloat16
F16 = mybir.dt.float16
F32 = mybir.dt.float32
I32 = mybir.dt.int32
U32 = mybir.dt.uint32

P = 128
SLOTS = 24
CHUNKS = 10
LAYERS = 3
ALPHA = 0.2
EPS = 1e-5
TINY = 1e-20
BIG = 3e38
EXP_LSB = 23
EXP_MASK = 0x7F800000


def gat_preln_kernel(nc, x, adj, W, a1, a2, out):
    N, D = x.shape
    H, _, F = W.shape
    T = N // P
    KT = D // P
    HF = H * F
    WORDS = 512
    SLICES = N // WORDS
    EDGES = CHUNKS * P
    ROW = HF + H
    XW = SLOTS + H + 1
    GROUP = 3
    BANKS = -(-CHUNKS // GROUP)
    EXPW = P + XW
    HALF = HF // 2
    assert N % (2 * P) == 0 and D % P == 0 and BANKS <= 4 and HF == 512 and SLICES * WORDS == N and GROUP * EXPW <= 512

    table = nc.dram_tensor("node_table", [N, ROW], F32, kind="Internal").ap()
    w_view = W.rearrange("(s h) (k p) f -> p k s h f", p=P, s=2)

    with ExitStack() as ctx:
        def sb(name, shape, dt):
            return ctx.enter_context(nc.sbuf_tensor(name, shape, dt))

        def sem(name):
            return ctx.enter_context(nc.semaphore(name))

        psum = ctx.enter_context(nc.psum_tensor("psum", [P, 8, 512], F32))
        bank = [psum[:, i, :] for i in range(8)]
        words_ps, turned_ps = bank[0:2], bank[2:4]
        h_ps = [psum[:, 4:6, :], psum[:, 6:8, :]]
        expand_ps = psum[:, 0:BANKS, :]
        sum_ps = [psum[:, 4:6, :], psum[:, 6:8, :]]

        ident = sb("ident", [P, P], F32)
        ident_b = sb("ident_b", [P, P], BF16)
        weigh = sb("weigh", [P, SLICES, P], BF16)
        before = sb("before", [P, P], BF16)
        ones_f = sb("ones_f", [P, P], F32)
        ones2 = sb("ones2", [2, P], BF16)
        low_bits = sb("low_bits", [2, WORDS], F32)
        high_bit = sb("high_bit", [2, WORDS], F32)
        column = sb("column", [2, WORDS], BF16)
        edge_no = sb("edge_no", [P, EDGES], F16)
        edge_less_slot = sb("edge_less_slot", [P, CHUNKS, SLOTS], F32)
        w_sb = sb("w_sb", [P, KT, 2, HALF + H], F32)
        a_sb = sb("a_sb", [P, 2, HF], F32)
        eps = sb("eps", [P, 1], F32)
        minus1 = sb("minus1", [P, 1], F32)

        adj_sb = sb("adj_sb", [P, 3, N], I32)
        mask = sb("mask", [P, 2, N], BF16)
        gath = [adj_sb[:, b, 0:CHUNKS * ROW].bitcast(F32).rearrange("p (c w) -> p c w", c=CHUNKS) for b in range(3)]
        mask_flat = mask[:].rearrange("p b n -> p (b n)")
        row_of = [mask_flat[:, b * 2 * CHUNKS * EXPW:(b + 1) * 2 * CHUNKS * EXPW].bitcast(F32)
                  .rearrange("p (c w) -> p c w", c=CHUNKS) for b in range(3)]
        pick = [mask_flat[:, 6 * CHUNKS * EXPW + b * EDGES:6 * CHUNKS * EXPW + (b + 1) * EDGES] for b in range(2)]

        class dense:
            pass
        taken = [0, 0]

        def dense_tensor(b, *shape):
            n = int(shape[0] if len(shape) == 1 else shape[0] * shape[1])
            at = adj_sb[:, b, taken[b]:taken[b] + n]
            taken[b] += n
            at = at.bitcast(F32)
            return at if len(shape) == 1 else at.rearrange("p (h m) -> p h m", m=shape[1])

        dense.diag, dense.a, dense.b = (dense_tensor(0, H, P) for _ in range(3))
        dense.mask, dense.barred = dense_tensor(0, P), dense_tensor(0, P)
        dense.acc, dense.nodes = dense_tensor(0, HF), dense_tensor(0, ROW)
        dense.x, dense.out, dense.att, dense.neg_att, dense.exp_att = (dense_tensor(1, HF) for _ in range(5))
        dense.top, dense.den, dense.part, dense.s1, dense.most = (dense_tensor(1, H) for _ in range(5))
        dense.alone, dense.adj = dense_tensor(1, 1), dense_tensor(1, P).bitcast(I32)

        x_sb = sb("x_sb", [P, 3, D], F32)
        stats = sb("stats", [P, 2, 6], F32)
        mean_var = sb("mean_var", [P, 2, 2], F32)
        std = sb("std", [P, 2, 1], F32)
        rstd = sb("rstd", [P, 2, 1], F32)
        shift = sb("shift", [P, 2, 1], F32)
        hn = sb("hn", [P, 2, D], F32)
        hn_t = sb("hn_t", [P, 2, D], F32)
        row_sb = sb("row_sb", [P, 3, ROW], F32)
        s2_top = sb("s2_top", [P, H], F32)
        left1 = sb("left1", [P, WORDS], F32)
        left2 = sb("left2", [P, WORDS], F32)
        keys = sb("keys", [P, SLOTS], F32)
        keys_i = sb("keys_i", [P, SLOTS], I32)
        col_i = sb("col_i", [P, SLOTS], I32)
        col_f = sb("col_f", [P, SLOTS], F32)
        high = sb("high", [P, LAYERS, SLOTS], F32)
        rest = sb("rest", [P, LAYERS, SLOTS], F32)
        expo = sb("expo", [P, LAYERS * SLOTS], I32)
        cand = sb("cand", [P, LAYERS * SLOTS], F32)
        cand1 = sb("cand1", [P, LAYERS * SLOTS], F32)
        cand2 = sb("cand2", [P, LAYERS * SLOTS], F32)
        list_sb = sb("list_sb", [P, SLOTS], F32)
        positive = sb("positive", [P, SLOTS], F32)

        values = sb("values", [P, T, XW], F32)
        adj_sum = sb("adj_sum", [P, T], F32)
        degree = sb("degree", [P, T], F32)
        degree_b = sb("degree_b", [P, T], BF16)
        first_edge = sb("first_edge", [P, T], F32)
        neg_middle = sb("neg_middle", [P, T], F32)
        reach = sb("reach", [P, T], F32)
        part = [sb(f"part{i}", [P, T, XW], BF16) for i in range(2)]
        part2 = sb("part2", [P, T, H], BF16)
        resid = sb("resid", [P, T, H], F32)
        ok = sb("ok", [P, 4], F32)
        okays = sb("okays", [P, T], F32)
        den_ok = sb("den_ok", [P, T, H], F32)
        s2_max1 = sb("s2_max1", [H, 1], F32)
        s2_diag = sb("s2_diag", [H, H], F32)
        s2_max = sb("s2_max", [P, H], F32)
        verdict = sb("verdict", [P, 1], I32)

        off = sb("off", [P, 2, EDGES], F16)
        match = sb("match", [P, CHUNKS, SLOTS], F32)
        chosen = sb("chosen", [P, CHUNKS, SLOTS], F32)
        back = sb("back", [P, CHUNKS], F32)
        index = sb("index", [P, 2, CHUNKS], U32)
        z = sb("z", [P, CHUNKS, H], F32)
        zl = sb("zl", [P, CHUNKS, H], F32)
        zmax = sb("zmax", [P, CHUNKS, H], F32)
        zml = sb("zml", [P, CHUNKS, H], F32)
        score = sb("score", [P, 2, CHUNKS, H], F32)
        den = sb("den", [P, H], F32)
        rden = sb("rden", [P, H], F32)
        att = sb("att", [P, 2, HF], F32)
        exp_att = sb("exp_att", [P, 2, HF], F32)
        res = sb("res", [P, 2, HF], F32)
        res1 = sb("res1", [P, HF], F32)
        out_sb = sb("out_sb", [P, 2, HF], F32)

        pool_const, dve_const = sem("pool_const"), sem("dve_const")
        w_landed, a1_landed, a2_landed = sem("w_landed"), sem("a1_landed"), sem("a2_landed")
        adj_landed = [sem(f"adj_landed{b}") for b in range(3)]
        x_landed = [sem(f"x_landed{b}") for b in range(3)]
        row_stored = [sem(f"row_stored{b}") for b in range(3)]
        mask_done, words_packed, words_read = sem("mask_done"), sem("words_packed"), sem("words_read")
        var_done, std_done, shift_done, hn_done = sem("var_done"), sem("std_done"), sem("shift_done"), sem("hn_done")
        hn_turned, hn_t_done, h_done = sem("hn_turned"), sem("hn_t_done"), sem("h_done")
        h_copied, s2_maxed = sem("h_copied"), sem("s2_maxed")
        extract_begun, listed = sem("extract_begun"), sem("listed")
        step = sem("step")
        prep_step, prep_pe, prep_ready = sem("prep_step"), sem("prep_pe"), sem("prep_ready")
        middle_ready = sem("middle_ready")
        gath_zeroed, gather_begun = sem("gath_zeroed"), sem("gather_begun")
        off_done, pick_done, expanded, row_of_done, index_done = (
            sem("off_done"), sem("pick_done"), sem("expanded"), sem("row_of_done"), sem("index_done"))
        gathered = [sem(f"gathered{b}") for b in range(3)]
        score_done, prob_done, weighted, act_weighted, aggregated = (
            sem("score_done"), sem("prob_done"), sem("weighted"), sem("act_weighted"), sem("aggregated"))
        x2_landed = [sem(f"x2_landed{b}") for b in range(3)]
        att_done, exp_done, res_done, out_done = sem("att_done"), sem("exp_done"), sem("res_done"), sem("out_done")
        out_stored = [sem(f"out_stored{b}") for b in range(2)]
        verdict_step, verdict_pe = sem("verdict_step"), sem("verdict_pe")
        dense_free, dense_tile, dense_landed, dense_x_landed, dense_stored = (
            sem("dense_free"), sem("dense_tile"), sem("dense_landed"), sem("dense_x_landed"), sem("dense_stored"))
        dense_diag, dense_spread, dense_arg, dense_exp_done, dense_prob = (
            sem("dense_diag"), sem("dense_spread"), sem("dense_arg"), sem("dense_exp_done"), sem("dense_prob"))
        dense_begun = sem("dense_begun")
        dense_turned, dense_copied, dense_summed = sem("dense_turned"), sem("dense_copied"), sem("dense_summed")
        dense_att, dense_elu, dense_out_done = sem("dense_att"), sem("dense_elu"), sem("dense_out_done")

        UNROLL = 6
        assert T % UNROLL == 0
        MULT_DVE = 7
        DVE_PARTS = ((0, 2), (2, 4), (4, MULT_DVE))
        LOG_WORDS = WORDS.bit_length() - 1
        EARLY = T - UNROLL
        DEGREE_READY, DIAG_READY = (1, 11), 22

        def rows(ap, t):
            return ap[bass.ts(t, P), :]

        def each_tile(eng, step, last_lag):
            for t in range(UNROLL):
                step(t // UNROLL, t % UNROLL, lambda k: 0 <= t - k < T)
            with eng.Fori(1, T // UNROLL - 1) as i:
                for r in range(UNROLL):
                    step(i, r, lambda k: True)
            for t in range(T - UNROLL, T + last_lag):
                step(t // UNROLL, t % UNROLL, lambda k: 0 <= t - k < T)

        def landed(i, r, lag, buffers, each=16):
            return each * (i * (UNROLL // buffers) + (r - lag) // buffers + 1)

        block = ctx.enter_context(nc.Block())

        def must_go_dense(eng):
            eng.wait_ge(verdict_step, 3)
            for b in range(2):
                eng.wait_ge(out_stored[b], 16 * (T // 2))
            return eng.value_load(verdict[0:1, 0:1], min_val=0, max_val=P) < P

        def all_visits(eng, before_tile, visit, between, after_tile):
            with eng.Fori(0, T) as t:
                before_tile(t)
                with eng.Fori(0, T) as c:
                    visit(t * (2 * T) + c, t, 0, c)
                between(t)
                with eng.Fori(0, T) as c:
                    visit(t * (2 * T) + c + T, t, 1, c)
                after_tile(t)

        def nothing(t):
            pass

        @block.sync
        def _(sp):
            def load(i, r, has):
                t = UNROLL * i + r
                if has(3):
                    sp.wait_ge(mask_done, t - 2)
                sp.dma_start(adj_sb[:, r % 3, :], rows(adj, t)).then_inc(adj_landed[r % 3], 16)
                if has(-2):
                    if has(1):
                        sp.wait_ge(hn_done, t)
                    sp.dma_start(x_sb[:, (r + 2) % 3, :], rows(x, t + 2)).then_inc(x_landed[(r + 2) % 3], 16)
            for t in range(2):
                sp.dma_start(x_sb[:, t, :], rows(x, t)).then_inc(x_landed[t], 16)
            for k in range(KT):
                for half in range(2):
                    sp.dma_start(w_sb[:, k, half, 0:HALF].rearrange("p (h f) -> p h f", f=F),
                                 w_view[:, k, half]).then_inc(w_landed, 16)
            sp.dma_start(a_sb[:, 0, :], a1.rearrange("h f -> (h f)").partition_broadcast(P)).then_inc(a1_landed, 16)
            sp.dma_start(a_sb[:, 1, :], a2.rearrange("h f -> (h f)").partition_broadcast(P)).then_inc(a2_landed, 16)

            each_tile(sp, load, 0)

            sp.wait_ge(hn_done, T)

            def residual(i, r, has):
                t = UNROLL * i + r
                if has(0):
                    if has(3):
                        sp.wait_ge(res_done, t - 2)
                    sp.dma_start(x_sb[:, r % 3, :], rows(x, t)).then_inc(x2_landed[r % 3], 16)
                if has(4):
                    sp.wait_ge(out_done, t - 3)
                    sp.dma_start(rows(out, t - 4), out_sb[:, r % 2, :]).then_inc(out_stored[r % 2], 16)
            each_tile(sp, residual, 4)
            for b in range(2):
                sp.wait_ge(out_stored[b], 16 * (T // 2))

            def dense_x(t):
                sp.wait_ge(dense_tile, t + 1)
                sp.sem_inc(dense_begun, 1)
                sp.dma_start(dense.x, rows(x, t)).then_inc(dense_x_landed, 16)

            def dense_load(v, t, second, c):
                sp.wait_ge(dense_free, v + 1)
                sp.sem_inc(dense_begun, 1)
                sp.dma_start(dense.adj, adj[bass.ts(t, P), bass.ts(c, P)]).then_inc(dense_landed, 16)
                sp.dma_start(dense.nodes, rows(table, c)).then_inc(dense_landed, 16)

            def dense_store(t):
                sp.wait_ge(dense_out_done, t + 1)
                sp.sem_inc(dense_begun, 1)
                sp.dma_start(rows(out, t), dense.out).then_inc(dense_stored, 16)
                sp.wait_ge(dense_stored, (t + 1) * 16)
                sp.sem_inc(dense_begun, 1)

            with sp.If(must_go_dense(sp)):
                all_visits(sp, dense_x, dense_load, nothing, dense_store)

        @block.gpsimd
        def _(pool):
            nc.gpsimd.memset(ones_f[:], 1.0).then_inc(pool_const, 1)
            nc.gpsimd.memset(ones2[:], 1.0).then_inc(pool_const, 1)
            nc.gpsimd.memset(eps[:], EPS).then_inc(pool_const, 1)
            nc.gpsimd.memset(minus1[:], -1.0).then_inc(pool_const, 1)
            nc.gpsimd.memset(s2_top[:], -BIG).then_inc(pool_const, 1)
            nc.gpsimd.iota(low_bits[:], [[0, WORDS // 256], [-1, 256]], base=255, channel_multiplier=0,
                           allow_small_or_imprecise_dtypes=True).then_inc(pool_const, 1)
            nc.gpsimd.iota(high_bit[:], [[-256, WORDS // 256], [0, 256]], base=WORDS - 256, channel_multiplier=0,
                           allow_small_or_imprecise_dtypes=True).then_inc(pool_const, 1)
            nc.gpsimd.iota(edge_no[:], [[1, EDGES]], base=0, channel_multiplier=0,
                           allow_small_or_imprecise_dtypes=True).then_inc(pool_const, 1)
            nc.gpsimd.iota(edge_less_slot[:], [[P, CHUNKS], [-1, SLOTS]], base=0, channel_multiplier=1,
                           allow_small_or_imprecise_dtypes=True).then_inc(pool_const, 1)
            pool.wait_ge(pool_const, 9)
            nc.gpsimd.affine_select(out=ident[:], in_=ones_f[:], compare_op=ALU.is_equal, fill=0.0, base=0,
                                    pattern=[[-1, P]], channel_multiplier=1).then_inc(pool_const, 1)
            nc.gpsimd.affine_select(out=before[:], in_=ones_f[:], compare_op=ALU.is_gt, fill=0.0, base=0,
                                    pattern=[[1, P]], channel_multiplier=-1).then_inc(pool_const, 1)

            def store_row(i, r, has):
                t = UNROLL * i + r
                if has(1):
                    pool.wait_ge(h_copied, t)
                    b = (r - 1) % 3
                    pool.dma_start(rows(table, t - 1), row_sb[:, b, :]).then_inc(row_stored[b], 16)
                if not has(-3) and has(0):
                    pool.wait_ge(mask_done, t + 1)
                    nc.gpsimd.memset(gath[r % 3], 0.0).then_inc(gath_zeroed, 1)
            each_tile(pool, store_row, 1)

            pool.wait_ge(gath_zeroed, 3)
            for b in range(3):
                pool.wait_ge(row_stored[b], 16 * (T // 3))

            def gather(i, r, has):
                t = UNROLL * i + r
                pool.wait_ge(index_done, t + 1)
                if has(3):
                    pool.wait_ge(aggregated, t - 2)
                pool.sem_inc(gather_begun, 1)
                for c in range(CHUNKS):
                    nc.gpsimd.indirect_dma_start(
                        gath[r % 3][:, c, :], None, table, bass.IndirectOffsetOnAxis(index[:, r % 2, c:c + 1], 0),
                        bounds_check=N - 1, oob_is_err=False).then_inc(gathered[r % 3], 16)
            each_tile(pool, gather, 0)

        @block.scalar
        def _(act):
            def distances(t, r, used):
                if used:
                    act.wait_ge(pick_done, t - 1)
                nc.scalar.activation(off[:, r % 2, :], edge_no[:], ACT.Abs,
                                     bias=neg_middle[:, bass.ds(t, 1)]).then_inc(off_done, 1)

            def copy_expanded(t, r, used):
                act.wait_ge(expanded, t + 1)
                if used:
                    act.wait_ge(aggregated, t - 2)
                full, left = CHUNKS // GROUP, CHUNKS % GROUP
                wide = lambda ap: ap.rearrange("p g (c w) -> p g c w", w=EXPW)
                last = nc.scalar.copy(row_of[r % 3][:, 0:full * GROUP, :].rearrange("p (g c) w -> p g c w", g=full),
                                      wide(expand_ps[:, 0:full, 0:GROUP * EXPW]))
                if left:
                    last = nc.scalar.copy(row_of[r % 3][:, full * GROUP:CHUNKS, :],
                                          wide(expand_ps[:, full:full + 1, 0:left * EXPW])[:, 0])
                last.then_inc(row_of_done, 1)

            def node_step(i, r, has):
                t = UNROLL * i + r
                if not has(0):
                    act.wait_ge(middle_ready, 1)
                    distances(0, 0, False)
                    distances(1, 1, False)
                if has(0):
                    b = r % 2
                    act.wait_ge(shift_done, t + 1)
                    if has(2):
                        act.wait_ge(hn_turned, t - 1)
                    nc.scalar.activation(hn[:, b, :], x_sb[:, r % 3, :], ACT.Relu, scale=rstd[:, b, :],
                                         bias=shift[:, b, :]).then_inc(hn_done, 1)
                if has(-1):
                    b = (r + 1) % 2
                    act.wait_ge(var_done, t + 2)
                    nc.scalar.activation(std[:, b, :], mean_var[:, b, 1:2], ACT.Sqrt, bias=eps[:]).then_inc(std_done, 1)
                if has(0):
                    act.wait_ge(adj_landed[r % 3], landed(i, r, 0, 3))
                    if has(2):
                        act.wait_ge(words_packed, t - 1)
                    nc.scalar.activation(mask[:, r % 2, :], adj_sb[:, r % 3, :], ACT.Relu,
                                         accum_out=adj_sum[:, bass.ds(t, 1)]).then_inc(mask_done, 1)
                    act.wait_ge(hn_turned, t + 1)
                    if has(2):
                        act.wait_ge(h_done, t - 1)
                    nc.scalar.copy(hn_t[:, r % 2, :], turned_ps[r % 2][:]).then_inc(hn_t_done, 1)
                if has(1):
                    b = (r + 1) % 2
                    act.wait_ge(h_done, t)
                    to = (r - 1) % 3
                    if has(4):
                        act.wait_ge(row_stored[to], landed(i, r, 4, 3))
                        act.wait_ge(s2_maxed, t - 3)
                    nc.scalar.copy(values[:, bass.ds(t - 1, 1), SLOTS + 1:XW], h_ps[b][:, 0:1, HALF:HALF + H])
                    nc.scalar.copy(row_sb[:, to, HF:ROW], h_ps[b][:, 1, HALF:HALF + H])
                    nc.scalar.copy(row_sb[:, to, 0:HF].rearrange("p (s w) -> p s w", s=2),
                                   h_ps[b][:, :, 0:HALF]).then_inc(h_copied, 1)

            act.wait_ge(pool_const, 11)
            act.wait_ge(var_done, 1)
            nc.scalar.activation(std[:, 0, :], mean_var[:, 0, 1:2], ACT.Sqrt, bias=eps[:]).then_inc(std_done, 1)
            each_tile(act, node_step, 1)

            copy_expanded(0, 0, False)
            distances(2, 2, True)
            distances(3, 3, True)
            act.wait_ge(middle_ready, 2)

            def weigh_chunk(b, c):
                for head in range(H):
                    piece = gath[b][:, c, head * F:(head + 1) * F]
                    last = nc.scalar.mul(piece, piece, gath[b][:, c, HF + head:HF + head + 1])
                last.then_inc(act_weighted, 1)

            def edge_step(i, r, has):
                t = UNROLL * i + r
                if has(1):
                    b = (r - 1) % 3
                    act.wait_ge(score_done, t)
                    act.wait_ge(gathered[b], landed(i, r, 1, 3, 16 * CHUNKS))
                    nc.scalar.activation(gath[b][:, :, HF:ROW], score[:, (r - 1) % 2], ACT.Exp).then_inc(prob_done, 1)
                    act.wait_ge(prob_done, t)
                    weigh_chunk(b, MULT_DVE)
                if has(-1):
                    copy_expanded(t + 1, r + 1, has(2))
                if has(1):
                    for c in range(MULT_DVE + 1, CHUNKS):
                        weigh_chunk((r - 1) % 3, c)
                if has(-4):
                    distances(t + 4, r + 4, True)
                if has(2):
                    act.wait_ge(att_done, t - 1)
                    if has(4):
                        act.wait_ge(res_done, t - 3)
                    nc.scalar.activation(exp_att[:, r % 2, :], att[:, r % 2, :], ACT.Exp).then_inc(exp_done, 1)
                if has(3):
                    b = (r + 1) % 2
                    act.wait_ge(res_done, t - 2)
                    if has(5):
                        act.wait_ge(out_stored[b], landed(i, r, 5, 2))
                    nc.scalar.activation(out_sb[:, b, :], res[:, b, :], ACT.Identity,
                                         bias=minus1[:]).then_inc(out_done, 1)
            each_tile(act, edge_step, 3)

            def dense_exp(v, t, second, c):
                if second:
                    act.wait_ge(dense_arg, t * T + c + 1)
                    nc.scalar.activation(dense.b, dense.b, ACT.Exp).then_inc(dense_exp_done, 1)

            def dense_elu_exp(t):
                act.wait_ge(dense_att, t + 1)
                nc.scalar.activation(dense.exp_att, dense.neg_att, ACT.Exp).then_inc(dense_elu, 1)

            with act.If(must_go_dense(act)):
                all_visits(act, nothing, dense_exp, nothing, dense_elu_exp)

        @block.vector
        def _(dve):
            dve.wait_ge(pool_const, 11)
            nc.vector.tensor_copy(ident_b[:], ident[:]).then_inc(dve_const, 1)
            for j in range(SLICES):
                nc.vector.tensor_scalar(weigh[:, j, :], ident[:], float(WORDS << (SLICES - 1 - j)), None,
                                        ALU.mult).then_inc(dve_const, 1)
            nc.vector.tensor_scalar(low_bits[:], low_bits[:], ident[0:2, 0:1], None, ALU.mult).then_inc(dve_const, 1)
            dve.wait_ge(dve_const, SLICES + 2)
            nc.vector.scalar_tensor_tensor(out=column[:], in0=high_bit[:], scalar=ident[0:2, 1:2], in1=low_bits[:],
                                           op0=ALU.mult, op1=ALU.add).then_inc(dve_const, 1)
            dve.wait_ge(w_landed, 16 * 2 * KT)
            dve.wait_ge(a1_landed, 16)
            dve.wait_ge(a2_landed, 16)
            done = SLICES + 3
            for k in range(KT):
                for s in range(2):
                    scratch = hn[:, s, :]
                    nc.vector.tensor_tensor(scratch.rearrange("p (s w) -> p s w", s=2), w_sb[:, k, :, 0:HALF],
                                            a_sb[:, s, :].rearrange("p (s w) -> p s w", s=2),
                                            ALU.mult).then_inc(dve_const, 1)
                    dve.wait_ge(dve_const, done + 1)
                    nc.vector.tensor_reduce(w_sb[:, k, s, HALF:HALF + H], scratch.rearrange("p (h f) -> p h f", h=H),
                                            AX_X, ALU.add).then_inc(dve_const, 1)
                    dve.wait_ge(dve_const, done + 2)
                    done += 2

            def settle(n):
                dve.wait_ge(step, n)
                dve.sem_clear(step)

            def statistics(r, landings):
                dve.wait_ge(x_landed[r % 3], landings)
                nc.vector.bn_stats(stats[:, r % 2, :], x_sb[:, r % 3, :]).then_inc(step, 1)
                settle(1)
                nc.vector.bn_aggr(mean_var[:, r % 2, :], stats[:, r % 2, :]).then_inc(var_done, 1)

            def scale_shift(t, r, used):
                b = r % 2
                dve.wait_ge(std_done, t + 1)
                if used:
                    dve.wait_ge(hn_done, t - 1)
                nc.vector.reciprocal(rstd[:, b, :], std[:, b, :]).then_inc(step, 1)
                settle(1)
                nc.vector.scalar_tensor_tensor(out=shift[:, b, :], in0=mean_var[:, b, 0:1], scalar=-1.0,
                                               in1=rstd[:, b, :], op0=ALU.mult, op1=ALU.mult).then_inc(shift_done, 1)

            def extract(t, words):
                dve.wait_ge(words_packed, t + 1)
                dve.sem_inc(extract_begun, 1)
                nc.vector.max(keys[:, 0:8], words[:]).then_inc(step, 1)
                dve.wait_ge(step, 1)
                nc.vector.match_replace(left1[:], keys[:, 0:8], words[:], 0.0).then_inc(step, 1)
                dve.wait_ge(step, 2)
                dve.sem_inc(words_read, 1)
                nc.vector.max(keys[:, 8:16], left1[:]).then_inc(step, 1)
                dve.wait_ge(step, 3)
                nc.vector.match_replace(left2[:], keys[:, 8:16], left1[:], 0.0).then_inc(step, 1)
                dve.wait_ge(step, 4)
                nc.vector.max(keys[:, 16:24], left2[:]).then_inc(step, 1)
                dve.wait_ge(step, 5)
                exp_bits = lambda ap: ap.bitcast(I32)
                nc.vector.tensor_scalar(exp_bits(high[:, 0, :]), exp_bits(keys[:]), EXP_MASK, None,
                                        ALU.bitwise_and).then_inc(step, 1)
                nc.vector.tensor_copy(keys_i[:], keys[:]).then_inc(step, 1)
                dve.wait_ge(step, 7)
                nc.vector.tensor_tensor(rest[:, 1, :], keys[:], high[:, 0, :], ALU.subtract).then_inc(step, 1)
                nc.vector.tensor_scalar(col_i[:], keys_i[:], WORDS - 1, None, ALU.bitwise_and).then_inc(step, 1)
                dve.wait_ge(step, 9)
                nc.vector.tensor_scalar(exp_bits(high[:, 1, :]), exp_bits(rest[:, 1, :]), EXP_MASK, None,
                                        ALU.bitwise_and).then_inc(step, 1)
                nc.vector.tensor_scalar(col_f[:], col_i[:], float(1 - WORDS * (127 + LOG_WORDS)), None,
                                        ALU.add).then_inc(step, 1)
                dve.wait_ge(step, 11)
                nc.vector.tensor_tensor(rest[:, 2, :], rest[:, 1, :], high[:, 1, :],
                                        ALU.subtract).then_inc(step, 1)
                dve.wait_ge(step, 12)
                nc.vector.tensor_scalar(exp_bits(high[:, 2, :]), exp_bits(rest[:, 2, :]), EXP_MASK, None,
                                        ALU.bitwise_and).then_inc(step, 1)
                dve.wait_ge(step, 13)
                nc.vector.tensor_scalar(expo[:], exp_bits(high[:].rearrange("p l s -> p (l s)")), EXP_LSB, None,
                                        ALU.logical_shift_right).then_inc(step, 1)
                dve.wait_ge(step, 14)
                nc.vector.scalar_tensor_tensor(
                    out=cand[:].rearrange("p (l s) -> p l s", l=LAYERS), in0=expo[:].rearrange("p (l s) -> p l s", l=LAYERS),
                    scalar=float(WORDS), in1=col_f[:, None, :].broadcast_to([P, LAYERS, SLOTS]),
                    op0=ALU.mult, op1=ALU.add).then_inc(step, 1)
                dve.wait_ge(step, 15)
                nc.vector.max(list_sb[:, 0:8], cand[:]).then_inc(step, 1)
                dve.wait_ge(step, 16)
                nc.vector.match_replace(cand1[:], list_sb[:, 0:8], cand[:], -BIG).then_inc(step, 1)
                dve.wait_ge(step, 17)
                nc.vector.max(list_sb[:, 8:16], cand1[:]).then_inc(step, 1)
                dve.wait_ge(step, 18)
                nc.vector.match_replace(cand2[:], list_sb[:, 8:16], cand1[:], -BIG).then_inc(step, 1)
                dve.wait_ge(step, 19)
                nc.vector.max(list_sb[:, 16:24], cand2[:]).then_inc(step, 1)
                settle(20)
                nc.vector.tensor_scalar(positive[:], list_sb[:], 0.0, None, ALU.is_gt).then_inc(step, 1)
                nc.vector.tensor_scalar(values[:, bass.ds(t, 1), 0:SLOTS], list_sb[:, None, :], 0.0, None,
                                        ALU.max).then_inc(step, 1)
                settle(2)
                nc.vector.tensor_reduce(degree[:, bass.ds(t, 1)], positive[:], AX_X, ALU.add).then_inc(listed, 1)


            prepped = [0]

            def link(instruction):
                prepped[0] += 1
                instruction.then_inc(prep_step, 1)
                dve.wait_ge(prep_step, prepped[0])

            def split(t0, t1):
                link(nc.vector.tensor_copy(part[0][:, t0:t1, :], values[:, t0:t1, :]))
                link(nc.vector.tensor_tensor(part[1][:, t0:t1, 0:SLOTS + 1], values[:, t0:t1, 0:SLOTS + 1],
                                             part[0][:, t0:t1, 0:SLOTS + 1], ALU.subtract))
                link(nc.vector.tensor_tensor(resid[:, t0:t1, :], values[:, t0:t1, SLOTS + 1:XW],
                                             part[0][:, t0:t1, SLOTS + 1:XW], ALU.subtract))
                link(nc.vector.tensor_copy(part[1][:, t0:t1, SLOTS + 1:XW], resid[:, t0:t1, :]))
                nc.vector.tensor_tensor(part2[:, t0:t1, :], resid[:, t0:t1, :], part[1][:, t0:t1, SLOTS + 1:XW],
                                        ALU.subtract).then_inc(prep_ready, 1)

            def place(t0, t1, edges_before):
                nc.vector.tensor_copy(values[:, t0:t1, SLOTS], edges_before).then_inc(prep_step, 1)
                prepped[0] += 1
                link(nc.vector.tensor_copy(first_edge[:, t0:t1], edges_before))
                nc.vector.tensor_scalar(reach[:, t0:t1], degree[:, t0:t1], 0.5, -0.25, ALU.mult,
                                        ALU.add).then_inc(prep_step, 1)
                prepped[0] += 1
                link(nc.vector.scalar_tensor_tensor(out=neg_middle[:, t0:t1], in0=degree[:, t0:t1], scalar=-0.5,
                                                    in1=first_edge[:, t0:t1], op0=ALU.mult, op1=ALU.subtract))
                link(nc.vector.tensor_scalar(neg_middle[:, t0:t1], neg_middle[:, t0:t1], 0.5, None, ALU.add))
                dve.sem_inc(middle_ready, 1)

            def choose(t, r, used):
                dve.wait_ge(off_done, t + 1)
                if used:
                    dve.wait_ge(expanded, t - 1)
                nc.vector.tensor_scalar(pick[r % 2], off[:, r % 2, :], reach[:, bass.ds(t, 1)], None,
                                        ALU.is_le).then_inc(pick_done, 1)

            def select(t, r, indexed):
                mine = row_of[r % 3]
                dve.wait_ge(row_of_done, t + 1)
                nc.vector.tensor_tensor(match[:], edge_less_slot[:],
                                        mine[:, :, P + SLOTS:P + SLOTS + 1].broadcast_to([P, CHUNKS, SLOTS]),
                                        ALU.is_equal).then_inc(step, 1)
                dve.wait_ge(step, 1)
                nc.vector.tensor_tensor(chosen[:], match[:], mine[:, :, P:P + SLOTS], ALU.mult).then_inc(step, 1)
                dve.wait_ge(step, 2)
                nc.vector.tensor_reduce(back[:], chosen[:], AX_X, ALU.add).then_inc(step, 1)
                settle(3)
                if indexed is not None:
                    dve.wait_ge(*indexed)
                nc.vector.tensor_scalar(index[:, r % 2, :], back[:], -1.0, float(N), ALU.mult,
                                        ALU.add).then_inc(index_done, 1)

            def node_step(i, r, has):
                t = UNROLL * i + r
                if not has(-1) and has(0):
                    dve.wait_ge(listed, EARLY)
                    link(nc.vector.tensor_copy(degree_b[:, 0:EARLY], degree[:, 0:EARLY]))
                    assert prepped[0] == DEGREE_READY[0]
                if not has(0):
                    dve.wait_ge(prep_pe, 1)
                    place(0, EARLY, turned_ps[0][:, 0:EARLY])
                    split(0, UNROLL)
                    dve.wait_ge(words_packed, T)
                    choose(0, 0, False)
                if has(-1):
                    scale_shift(t + 1, r + 1, has(1))
                if has(-2):
                    statistics(r + 2, landed(i, r, -2, 3))
                if has(1):
                    b = (r + 1) % 2
                    extract(t - 1, words_ps[b])
                    dve.wait_ge(h_copied, t)
                    if has(2):
                        dve.wait_ge(s2_maxed, t - 1)
                    nc.vector.tensor_tensor(s2_top[:], row_sb[:, (r - 1) % 3, HF:ROW], s2_top[:],
                                            ALU.max).then_inc(s2_maxed, 1)

            statistics(0, 16)
            scale_shift(0, 0, False)
            statistics(1, 16)
            each_tile(dve, node_step, 1)

            def weigh_part(b, c0, c1):
                piece = gath[b][:, c0:c1, 0:HF].rearrange("p c (h f) -> p c h f", h=H)
                nc.vector.tensor_tensor(piece, piece, gath[b][:, c0:c1, HF:ROW, None].broadcast_to([P, c1 - c0, H, F]),
                                        ALU.mult).then_inc(weighted, 1)

            def edge_step(i, r, has):
                t = UNROLL * i + r
                if has(1):
                    b = (r - 1) % 3
                    dve.wait_ge(gathered[b], landed(i, r, 1, 3, 16 * CHUNKS))
                    s1_e = row_of[b][:, :, P + SLOTS + 1:EXPW]
                    nc.vector.tensor_tensor(z[:], s1_e, gath[b][:, :, HF:ROW], ALU.add).then_inc(step, 1)
                    nc.vector.tensor_tensor(zmax[:], s1_e, s2_max[:, None, :].broadcast_to([P, CHUNKS, H]),
                                            ALU.add).then_inc(step, 1)
                    dve.wait_ge(step, 2)
                    nc.vector.scalar_tensor_tensor(out=zl[:], in0=z[:], scalar=ALPHA, in1=z[:], op0=ALU.mult,
                                                   op1=ALU.max).then_inc(step, 1)
                    nc.vector.scalar_tensor_tensor(out=zml[:], in0=zmax[:], scalar=ALPHA, in1=zmax[:], op0=ALU.mult,
                                                   op1=ALU.max).then_inc(step, 1)
                    settle(4)
                    if has(3):
                        dve.wait_ge(prob_done, t - 2)
                    nc.vector.tensor_tensor(score[:, (r - 1) % 2], zl[:], zml[:], ALU.subtract).then_inc(score_done, 1)
                if has(1):
                    dve.wait_ge(prob_done, t)
                    for c0, c1 in DVE_PARTS:
                        weigh_part(b, c0, c1)
                if has(-3):
                    choose(t + 3, r + 3, True)
                if has(-1):
                    used = (gathered[(r - 1) % 3], landed(i, r, 1, 3, 16 * CHUNKS)) if has(1) else None
                    select(t + 1, r + 1, used)
                if has(2):
                    b = r % 2
                    den_ps = sum_ps[b][:, 1, HALF:HALF + H]
                    dve.wait_ge(aggregated, t - 1)
                    nc.vector.tensor_scalar(den_ok[:, bass.ds(t - 2, 1), :], den_ps[:, None, :], TINY, None,
                                            ALU.is_ge).then_inc(step, 1)
                    nc.vector.tensor_scalar(den[:], den_ps, TINY, None, ALU.max).then_inc(step, 1)
                    dve.wait_ge(step, 2)
                    nc.vector.reciprocal(rden[:], den[:]).then_inc(step, 1)
                    settle(3)
                    if has(4):
                        dve.wait_ge(exp_done, t - 3)
                    heads = lambda ap: ap.rearrange("p s (h f) -> p s h f", f=F)
                    nc.vector.tensor_tensor(
                        heads(att[:, b, :].rearrange("p (s w) -> p s w", s=2)), heads(sum_ps[b][:, :, 0:HALF]),
                        rden[:].rearrange("p (s h) -> p s h", s=2)[:, :, :, None].broadcast_to([P, 2, H // 2, F]),
                        ALU.mult).then_inc(att_done, 1)
                if has(3):
                    b = (r + 1) % 2
                    dve.wait_ge(exp_done, t - 2)
                    dve.wait_ge(x2_landed[r % 3], landed(i, r, 3, 3))
                    if has(4):
                        dve.wait_ge(res_done, t - 3)
                    nc.vector.scalar_tensor_tensor(out=res1[:], in0=exp_att[:, b, :], scalar=1.0, in1=x_sb[:, r % 3, :],
                                                   op0=ALU.min, op1=ALU.add).then_inc(step, 1)
                    settle(1)
                    if has(5):
                        dve.wait_ge(out_done, t - 4)
                    nc.vector.scalar_tensor_tensor(out=res[:, b, :], in0=att[:, b, :], scalar=0.0, in1=res1[:],
                                                   op0=ALU.max, op1=ALU.add).then_inc(res_done, 1)

            select(0, 0, None)
            choose(1, 1, False)
            dve.wait_ge(listed, T)
            link(nc.vector.tensor_copy(degree_b[:, EARLY:T], degree[:, EARLY:T]))
            assert prepped[0] == DEGREE_READY[1]
            choose(2, 2, True)
            dve.wait_ge(prep_pe, 3)
            place(EARLY, T, bank[5][:, 0:T - EARLY])
            dve.wait_ge(h_copied, T)
            split(UNROLL, T)
            link(nc.vector.tensor_reduce(s2_max1[:], bank[4][0:H, 0:P], AX_X, ALU.max))
            link(nc.vector.tensor_scalar(s2_diag[:], ident[0:H, 0:H], s2_max1[:], None, ALU.mult))
            assert prepped[0] == DIAG_READY
            dve.wait_ge(prep_pe, 4)
            link(nc.vector.tensor_copy(s2_max[:], bank[6][:, 0:H]))
            each_tile(dve, edge_step, 3)

            link(nc.vector.tensor_tensor(okays[:], degree[:], adj_sum[:], ALU.is_equal))
            link(nc.vector.tensor_reduce(ok[:, 0:1], okays[:], AX_X, ALU.min))
            link(nc.vector.tensor_tensor(okays[:], degree[:], first_edge[:], ALU.add))
            link(nc.vector.tensor_scalar(okays[:], okays[:], float(EDGES), None, ALU.is_le))
            link(nc.vector.tensor_reduce(ok[:, 1:2], okays[:], AX_X, ALU.min))
            dve.wait_ge(att_done, T)
            nc.vector.tensor_reduce(ok[:, 2:3], den_ok[:].rearrange("p t h -> p (t h)"), AX_X,
                                    ALU.min).then_inc(verdict_step, 1)
            dve.wait_ge(verdict_step, 1)
            nc.vector.tensor_reduce(ok[:, 3:4], ok[:, 0:3], AX_X, ALU.min).then_inc(verdict_step, 1)
            dve.wait_ge(verdict_pe, 1)
            nc.vector.tensor_copy(verdict[0:1, :], expand_ps[0:1, 0, 0:1]).then_inc(verdict_step, 1)

            def over_nodes(ap):
                return ap[:, :, None].broadcast_to([P, H, P])

            def over_heads(ap):
                return ap[:, None, :].broadcast_to([P, H, P])

            def alone(instruction):
                instruction.then_inc(step, 1)
                settle(1)

            def dense_start(t):
                alone(nc.vector.memset(dense.top, -BIG))
                alone(nc.vector.memset(dense.den, 0.0))
                alone(nc.vector.memset(dense.acc, 0.0))

            def dense_visit(v, t, second, c):
                dve.wait_ge(dense_landed, (v + 1) * 32)
                nc.vector.tensor_tensor(dense.diag, over_heads(ident[:]), over_nodes(dense.nodes[:, HF:ROW]),
                                        ALU.mult).then_inc(dense_diag, 1)
                alone(nc.vector.tensor_scalar(dense.mask, dense.adj, 0.0, None, ALU.is_gt))
                dve.wait_ge(dense_spread, v + 1)
                for half in range(2):
                    alone(nc.vector.tensor_copy(dense.a[:, half * (H // 2):(half + 1) * (H // 2), :],
                                                bank[half][:].rearrange("p (h m) -> p h m", m=P)))
                if not second:
                    alone(nc.vector.tensor_scalar(dense.barred, dense.mask, -1.0, BIG, ALU.add, ALU.mult))
                    alone(nc.vector.tensor_tensor(dense.b, dense.a, over_heads(dense.mask), ALU.mult))
                    alone(nc.vector.tensor_tensor(dense.b, dense.b, over_heads(dense.barred), ALU.add))
                    alone(nc.vector.tensor_reduce(dense.part, dense.b, AX_X, ALU.max))
                    nc.vector.tensor_tensor(dense.top, dense.top, dense.part, ALU.max).then_inc(dense_free, 1)
                    return
                alone(nc.vector.tensor_tensor(dense.a, dense.a, over_nodes(dense.s1), ALU.add))
                alone(nc.vector.scalar_tensor_tensor(out=dense.b, in0=dense.a, scalar=ALPHA, in1=dense.a,
                                                     op0=ALU.mult, op1=ALU.max))
                alone(nc.vector.tensor_tensor(dense.b, dense.b, over_nodes(dense.most), ALU.subtract))
                nc.vector.tensor_scalar(dense.b, dense.b, 0.0, None, ALU.min).then_inc(dense_arg, 1)
                dve.wait_ge(dense_exp_done, t * T + c + 1)
                alone(nc.vector.tensor_tensor(dense.b, dense.b, over_heads(dense.mask), ALU.mult))
                nc.vector.tensor_scalar(dense.b, dense.b, dense.alone, None, ALU.add).then_inc(dense_prob, 1)
                dve.wait_ge(dense_prob, t * T + c + 1)
                alone(nc.vector.tensor_reduce(dense.part, dense.b, AX_X, ALU.add))
                alone(nc.vector.tensor_tensor(dense.den, dense.den, dense.part, ALU.add))
                dve.wait_ge(dense_turned, t * T + c + 1)
                for half in range(2):
                    last = nc.vector.tensor_copy(dense.diag[:, half * (H // 2):(half + 1) * (H // 2), :],
                                                 bank[2 + half][:].rearrange("p (h m) -> p h m", m=P))
                last.then_inc(dense_copied, 1)
                dve.wait_ge(dense_summed, t * T + c + 1)
                nc.vector.tensor_tensor(dense.acc, dense.acc, bank[4][:], ALU.add).then_inc(dense_free, 1)

            def dense_most(t):
                dve.wait_ge(dense_free, t * (2 * T) + T + 1)
                alone(nc.vector.tensor_copy(dense.s1[:, None, :], values[:, bass.ds(t, 1), SLOTS + 1:XW]))
                alone(nc.vector.tensor_tensor(dense.part, dense.s1, dense.top, ALU.add))
                alone(nc.vector.scalar_tensor_tensor(out=dense.most, in0=dense.part, scalar=ALPHA, in1=dense.part,
                                                     op0=ALU.mult, op1=ALU.max))
                alone(nc.vector.tensor_scalar(dense.alone, dense.top[:, 0:1], -BIG / 2, None, ALU.is_lt))

            def dense_finish(t):
                dve.wait_ge(dense_free, (t + 1) * (2 * T) + 1)
                alone(nc.vector.reciprocal(dense.part, dense.den))
                alone(nc.vector.tensor_tensor(dense.att.rearrange("p (h f) -> p h f", h=H),
                                              dense.acc.rearrange("p (h f) -> p h f", h=H),
                                              dense.part[:, :, None].broadcast_to([P, H, F]), ALU.mult))
                nc.vector.tensor_scalar(dense.neg_att, dense.att, 0.0, None, ALU.min).then_inc(dense_att, 1)
                dve.wait_ge(dense_elu, t + 1)
                alone(nc.vector.scalar_tensor_tensor(out=dense.att, in0=dense.att, scalar=0.0, in1=dense.exp_att,
                                                     op0=ALU.max, op1=ALU.add))
                dve.wait_ge(dense_x_landed, (t + 1) * 16)
                nc.vector.scalar_tensor_tensor(out=dense.out, in0=dense.att, scalar=-1.0, in1=dense.x,
                                               op0=ALU.add, op1=ALU.add).then_inc(dense_out_done, 1)
                dve.wait_ge(dense_stored, (t + 1) * 16)
                dve.sem_inc(dense_tile, 1)

            with dve.If(must_go_dense(dve)):
                dve.sem_inc(dense_free, 1)
                dve.sem_inc(dense_tile, 1)
                all_visits(dve, dense_start, dense_visit, dense_most, dense_finish)

        @block.tensor
        def _(pe):
            def node_step(i, r, has):
                t = UNROLL * i + r
                if has(1):
                    b = (r + 1) % 2
                    pe.wait_ge(hn_t_done, t)
                    if has(3):
                        pe.wait_ge(h_copied, t - 2)
                    for k in range(KT):
                        for half in range(2):
                            last = nc.tensor.matmul(h_ps[b][:, half, 0:HALF + H], hn_t[:, b, k * P:(k + 1) * P],
                                                    w_sb[:, k, half, :], start=(k == 0), stop=(k == KT - 1))
                    last.then_inc(h_done, 1)
                if has(0):
                    b = r % 2
                    pe.wait_ge(hn_done, t + 1)
                    if has(2):
                        pe.wait_ge(hn_t_done, t - 1)
                    for k in range(KT):
                        last = nc.tensor.transpose(turned_ps[b][:, k * P:(k + 1) * P], hn[:, b, k * P:(k + 1) * P], ident[:])
                    last.then_inc(hn_turned, 1)
                    if not has(-1):
                        pe.wait_ge(prep_step, DEGREE_READY[0])
                        nc.tensor.matmul(turned_ps[0][:, 0:EARLY], before[:], degree_b[:, 0:EARLY],
                                         start=True, stop=True).then_inc(prep_pe, 1)
                    pe.wait_ge(mask_done, t + 1)
                    if has(2):
                        pe.wait_ge(words_read, t - 1)
                    nc.tensor.matmul(words_ps[b][:], ones2[:], column[:], start=True, stop=False)
                    for j in range(SLICES):
                        last = nc.tensor.matmul(words_ps[b][:], weigh[:, j, :], mask[:, b, j * WORDS:(j + 1) * WORDS],
                                                start=False, stop=(j == SLICES - 1))
                    last.then_inc(words_packed, 1)

            pe.wait_ge(pool_const, 11)
            pe.wait_ge(w_landed, 16 * 2 * KT)
            pe.wait_ge(dve_const, SLICES + 3 + 4 * KT)
            each_tile(pe, node_step, 1)

            def expand(t, r, used):
                pe.wait_ge(pick_done, t + 1)
                if used:
                    pe.wait_ge(row_of_done, t)
                for c in range(CHUNKS):
                    one_hot = pick[r % 2][:, c * P:(c + 1) * P]
                    to = expand_ps[:, c // GROUP, (c % GROUP) * EXPW:(c % GROUP + 1) * EXPW]
                    nc.tensor.matmul(to[:, 0:P], one_hot, ident_b[:], start=True, stop=True)
                    nc.tensor.matmul(to[:, P:EXPW], one_hot, part[0][:, bass.ds(t, 1), :].rearrange("p a w -> p (a w)"),
                                     start=True, stop=False)
                    nc.tensor.matmul(to[:, P + SLOTS + 1:EXPW], one_hot,
                                     part2[:, bass.ds(t, 1), :].rearrange("p a w -> p (a w)"), start=False, stop=False)
                    last = nc.tensor.matmul(to[:, P:EXPW], one_hot,
                                            part[1][:, bass.ds(t, 1), :].rearrange("p a w -> p (a w)"),
                                            start=False, stop=True)
                last.then_inc(expanded, 1)

            def edge_step(i, r, has):
                t = UNROLL * i + r
                if has(1):
                    b, to = (r - 1) % 3, sum_ps[(r + 1) % 2]
                    if has(3):
                        pe.wait_ge(att_done, t - 2)
                    first_of = {c0: n for n, (c0, _) in enumerate(DVE_PARTS)}
                    for c in range(CHUNKS):
                        if c == MULT_DVE and has(-2):
                            expand(t + 2, r + 2, True)
                        if c in first_of:
                            pe.wait_ge(weighted, len(DVE_PARTS) * (t - 1) + first_of[c] + 1)
                        if c >= MULT_DVE:
                            pe.wait_ge(act_weighted, (CHUNKS - MULT_DVE) * (t - 1) + c - MULT_DVE + 1)
                        one_hot = row_of[b][:, c, 0:P]
                        nc.tensor.matmul(to[:, 0, 0:HALF], one_hot, gath[b][:, c, 0:HALF],
                                         start=(c == 0), stop=(c == CHUNKS - 1))
                        last = nc.tensor.matmul(to[:, 1, 0:HALF + H], one_hot, gath[b][:, c, HALF:ROW],
                                                start=(c == 0), stop=(c == CHUNKS - 1))
                    last.then_inc(aggregated, 1)
                elif has(-2):
                    expand(t + 2, r + 2, True)

            pe.wait_ge(prep_ready, 1)
            pe.wait_ge(words_read, T)
            expand(0, 0, False)
            pe.wait_ge(s2_maxed, T)
            nc.tensor.transpose(bank[4][0:H, 0:P], s2_top[:], ident[:]).then_inc(prep_pe, 1)
            expand(1, 1, True)
            pe.wait_ge(prep_step, DEGREE_READY[1])
            nc.tensor.matmul(bank[5][:, 0:T - EARLY], before[:], degree_b[:, EARLY:T], start=True,
                             stop=True).then_inc(prep_pe, 1)
            pe.wait_ge(prep_step, DIAG_READY)
            nc.tensor.matmul(bank[6][:, 0:H], ones_f[0:H, :], s2_diag[:], start=True, stop=True).then_inc(prep_pe, 1)
            pe.wait_ge(prep_ready, 2)
            each_tile(pe, edge_step, 1)

            pe.wait_ge(verdict_step, 2)
            nc.tensor.matmul(expand_ps[0:1, 0, 0:1], ok[:, 3:4], ones_f[:, 0:1], start=True, stop=True).then_inc(verdict_pe, 1)

            def dense_products(v, t, second, c):
                pe.wait_ge(dense_diag, v + 1)
                for half in range(2):
                    last = nc.tensor.matmul(bank[half][:], ones_f[:], dense.diag[:, half * (H // 2):(half + 1) * (H // 2), :]
                                            .rearrange("p h m -> p (h m)"), start=True, stop=True)
                last.then_inc(dense_spread, 1)
                if second:
                    pe.wait_ge(dense_prob, t * T + c + 1)
                    for h in range(H):
                        last = nc.tensor.transpose(bank[2 + h // (H // 2)][:, (h % (H // 2)) * P:(h % (H // 2) + 1) * P],
                                                   dense.b[:, h, :], ident[:])
                    last.then_inc(dense_turned, 1)
                    pe.wait_ge(dense_copied, t * T + c + 1)
                    for h in range(H):
                        last = nc.tensor.matmul(bank[4][:, h * F:(h + 1) * F], dense.diag[:, h, :],
                                                dense.nodes[:, h * F:(h + 1) * F], start=True, stop=True)
                    last.then_inc(dense_summed, 1)

            with pe.If(must_go_dense(pe)):
                all_visits(pe, nothing, dense_products, nothing, nothing)


def kernel(**inputs):
    import numpy as _np
    import concourse.bacc as _bacc
    from concourse import mybir as _mybir
    from concourse.bass_utils import run_bass_kernel_spmd as _run

    nc = _bacc.Bacc("TRN2", target_bir_lowering=False, num_devices=1)
    arrays, args = {}, []
    for name in ("x", "adj", "L0_gnn_W", "L0_gnn_a1", "L0_gnn_a2"):
        a = _np.ascontiguousarray(inputs[name])
        arrays[f"in_{name}"] = a
        args.append(nc.dram_tensor(f"in_{name}", a.shape, _mybir.dt.from_np(a.dtype), kind="ExternalInput").ap())
    out = nc.dram_tensor("out", inputs["x"].shape, _mybir.dt.float32, kind="ExternalOutput").ap()
    gat_preln_kernel(nc, *args, out)
    r = _run(nc, [arrays], core_ids=[0])
    return r.results[0]["out"]
```
